# Optimizing a Trainium2 kernel written in Bass

```python
import numpy as np
import jax
import jax.numpy as jnp

def _softmax(x, axis=-1):
    return jax.nn.softmax(x, axis=axis)

def _gelu(x):
    return jax.nn.gelu(x, approximate=True)

def _silu(x):
    return jax.nn.silu(x)

def _sigmoid(x):
    return jax.nn.sigmoid(x)

def _layernorm(x, axis=-1, eps=1e-05):
    m = jnp.mean(x, axis=axis, keepdims=True)
    v = jnp.var(x, axis=axis, keepdims=True)
    return (x - m) / jnp.sqrt(v + eps)

def _scatter_add(tgt, idx, src, axis=0):
    return tgt.at[idx].add(src)

def _segment_sum(src, seg, n):
    return jax.ops.segment_sum(src, seg, n)
kernel_name = 'mk_adaln_d1_jaxref_r8_ed7e6e'

def setup_inputs(seed: int=0):
    np.random.seed(seed)
    _w = jnp.asarray

    def _L0_attn_setup():
        import jax, jax.numpy as jnp
        import numpy as np
        D_MODEL = 128
        D_STATE = 16
        D_CONV = 4
        EXPAND = 2
        D_INNER = EXPAND * D_MODEL
        DT_RANK = (D_MODEL + 15) // 16
        BATCH = 2
        SEQ = 256
        EPS = 1e-05

        def _mamba_params(key, scale=0.02):
            ks = jax.random.split(key, 8)
            n = lambda k, s: jax.random.normal(k, s, jnp.float32) * scale
            return {'Win': n(ks[0], (2 * D_INNER, D_MODEL)), 'convw': n(ks[1], (D_INNER, 1, D_CONV)), 'convb': n(ks[2], (D_INNER,)), 'Wx': n(ks[3], (DT_RANK + 2 * D_STATE, D_INNER)), 'Wdt': n(ks[4], (D_INNER, DT_RANK)), 'bdt': n(ks[5], (D_INNER,)), 'Alog': jnp.log(jnp.tile(jnp.arange(1, D_STATE + 1, dtype=jnp.float32), (D_INNER, 1))), 'D': jnp.ones((D_INNER,), jnp.float32), 'Wout': n(ks[6], (D_MODEL, D_INNER))}

        def _mamba(x, Win, convw, convb, Wx, Wdt, bdt, Alog, Dp, Wout):
            B, L, _ = x.shape
            xz = jnp.einsum('bld,ed->ble', x, Win)
            u, z = jnp.split(xz, 2, axis=-1)
            uc = jnp.transpose(u, (0, 2, 1))
            uc = jnp.pad(uc, ((0, 0), (0, 0), (D_CONV - 1, 0)))
            uc = jax.lax.conv_general_dilated(uc, convw, (1,), 'VALID', feature_group_count=D_INNER)
            uc = uc + convb[None, :, None]
            u = jax.nn.silu(jnp.transpose(uc, (0, 2, 1)))
            xdbl = jnp.einsum('bld,ed->ble', u, Wx)
            dtr, Bm, Cm = jnp.split(xdbl, [DT_RANK, DT_RANK + D_STATE], axis=-1)
            dt = jax.nn.softplus(jnp.einsum('blr,dr->bld', dtr, Wdt) + bdt)
            A = -jnp.exp(Alog)

            def step(h, ins):
                dt_t, u_t, B_t, C_t = ins
                h = jnp.exp(dt_t[..., None] * A) * h + (dt_t * u_t)[..., None] * B_t[:, None, :]
                y_t = jnp.einsum('bdn,bn->bd', h, C_t)
                return (h, y_t)
            h0 = jnp.zeros((B, D_INNER, D_STATE), jnp.float32)
            xs = (jnp.moveaxis(dt, 1, 0), jnp.moveaxis(u, 1, 0), jnp.moveaxis(Bm, 1, 0), jnp.moveaxis(Cm, 1, 0))
            _, ys = jax.lax.scan(step, h0, xs)
            y = jnp.moveaxis(ys, 0, 1) + u * Dp
            y = y * jax.nn.silu(z)
            return jnp.einsum('bld,ed->ble', y, Wout)
        key = jax.random.key(seed)
        kx, kf, kb = jax.random.split(key, 3)
        inp = {'x': jax.random.normal(kx, (BATCH, SEQ, D_MODEL), jnp.float32), 'norm_g': jnp.ones((D_MODEL,), jnp.float32), 'norm_b': jnp.zeros((D_MODEL,), jnp.float32)}
        for pfx, k in (('f', kf), ('b', kb)):
            for name, v in _mamba_params(k).items():
                inp[f'{pfx}_{name}'] = v
        return inp
    _L0_attn_in = _L0_attn_setup()

    def _L0_ffn_setup():
        import jax, jax.numpy as jnp
        import numpy as np
        EXPERTS = 8
        TOP_K = 2

        def swiglu(x, w1, w2, w3):
            h = x @ w1
            return h * jax.nn.sigmoid(h) * (x @ w2) @ w3
        key = jax.random.key(seed)
        ks = jax.random.split(key, 9)
        B, S, D = (4, 256, 128)
        H = 2 * D
        s = 0.02
        x = jax.random.normal(ks[0], (B, S, D), dtype=jnp.float32)
        gate_w = jax.random.normal(ks[1], (D, EXPERTS), dtype=jnp.float32) * s
        ew1 = jax.random.normal(ks[2], (EXPERTS, D, H), dtype=jnp.float32) * s
        ew2 = jax.random.normal(ks[3], (EXPERTS, D, H), dtype=jnp.float32) * s
        ew3 = jax.random.normal(ks[4], (EXPERTS, H, D), dtype=jnp.float32) * s
        sw1 = jax.random.normal(ks[5], (D, H), dtype=jnp.float32) * s
        sw2 = jax.random.normal(ks[6], (D, H), dtype=jnp.float32) * s
        sw3 = jax.random.normal(ks[7], (H, D), dtype=jnp.float32) * s
        return {'x': x, 'gate_w': gate_w, 'ew1': ew1, 'ew2': ew2, 'ew3': ew3, 'sw1': sw1, 'sw2': sw2, 'sw3': sw3}
    _L0_ffn_in = _L0_ffn_setup()
    _L0_c = _w((lambda *s: np.random.randn(*s).astype(np.float32) * 0.05)(16, 128))
    _L0_wmod = _w((lambda *s: np.random.randn(*s).astype(np.float32) * 0.05)(128, 6 * 128) * 128 ** (-0.5))
    _d = {'L0_attn_x': _L0_attn_in['x'], 'L0_attn_norm_g': _L0_attn_in['norm_g'], 'L0_attn_norm_b': _L0_attn_in['norm_b'], 'L0_attn_f_Win': _L0_attn_in['f_Win'], 'L0_attn_f_convw': _L0_attn_in['f_convw'], 'L0_attn_f_convb': _L0_attn_in['f_convb'], 'L0_attn_f_Wx': _L0_attn_in['f_Wx'], 'L0_attn_f_Wdt': _L0_attn_in['f_Wdt'], 'L0_attn_f_bdt': _L0_attn_in['f_bdt'], 'L0_attn_f_Alog': _L0_attn_in['f_Alog'], 'L0_attn_f_D': _L0_attn_in['f_D'], 'L0_attn_f_Wout': _L0_attn_in['f_Wout'], 'L0_attn_b_Win': _L0_attn_in['b_Win'], 'L0_attn_b_convw': _L0_attn_in['b_convw'], 'L0_attn_b_convb': _L0_attn_in['b_convb'], 'L0_attn_b_Wx': _L0_attn_in['b_Wx'], 'L0_attn_b_Wdt': _L0_attn_in['b_Wdt'], 'L0_attn_b_bdt': _L0_attn_in['b_bdt'], 'L0_attn_b_Alog': _L0_attn_in['b_Alog'], 'L0_attn_b_D': _L0_attn_in['b_D'], 'L0_attn_b_Wout': _L0_attn_in['b_Wout'], 'L0_ffn_gate_w': _L0_ffn_in['gate_w'], 'L0_ffn_ew1': _L0_ffn_in['ew1'], 'L0_ffn_ew2': _L0_ffn_in['ew2'], 'L0_ffn_ew3': _L0_ffn_in['ew3'], 'L0_ffn_sw1': _L0_ffn_in['sw1'], 'L0_ffn_sw2': _L0_ffn_in['sw2'], 'L0_ffn_sw3': _L0_ffn_in['sw3'], 'L0_c': _L0_c, 'L0_wmod': _L0_wmod}
    _x0 = _d['L0_attn_x']
    _d['L0_attn_x'] = jax.random.normal(jax.random.fold_in(jax.random.key(seed), 1), (16, 512, 128), dtype=_x0.dtype)
    del _x0
    return _d

def reference(L0_attn_x, L0_attn_norm_g, L0_attn_norm_b, L0_attn_f_Win, L0_attn_f_convw, L0_attn_f_convb, L0_attn_f_Wx, L0_attn_f_Wdt, L0_attn_f_bdt, L0_attn_f_Alog, L0_attn_f_D, L0_attn_f_Wout, L0_attn_b_Win, L0_attn_b_convw, L0_attn_b_convb, L0_attn_b_Wx, L0_attn_b_Wdt, L0_attn_b_bdt, L0_attn_b_Alog, L0_attn_b_D, L0_attn_b_Wout, L0_ffn_gate_w, L0_ffn_ew1, L0_ffn_ew2, L0_ffn_ew3, L0_ffn_sw1, L0_ffn_sw2, L0_ffn_sw3, L0_c, L0_wmod):

    def _L0_attn_ref(x, norm_g, norm_b, f_Win, f_convw, f_convb, f_Wx, f_Wdt, f_bdt, f_Alog, f_D, f_Wout, b_Win, b_convw, b_convb, b_Wx, b_Wdt, b_bdt, b_Alog, b_D, b_Wout):
        import jax, jax.numpy as jnp
        import numpy as np
        D_MODEL = 128
        D_STATE = 16
        D_CONV = 4
        EXPAND = 2
        D_INNER = EXPAND * D_MODEL
        DT_RANK = (D_MODEL + 15) // 16
        BATCH = 2
        SEQ = 256
        EPS = 1e-05

        def _mamba_params(key, scale=0.02):
            ks = jax.random.split(key, 8)
            n = lambda k, s: jax.random.normal(k, s, jnp.float32) * scale
            return {'Win': n(ks[0], (2 * D_INNER, D_MODEL)), 'convw': n(ks[1], (D_INNER, 1, D_CONV)), 'convb': n(ks[2], (D_INNER,)), 'Wx': n(ks[3], (DT_RANK + 2 * D_STATE, D_INNER)), 'Wdt': n(ks[4], (D_INNER, DT_RANK)), 'bdt': n(ks[5], (D_INNER,)), 'Alog': jnp.log(jnp.tile(jnp.arange(1, D_STATE + 1, dtype=jnp.float32), (D_INNER, 1))), 'D': jnp.ones((D_INNER,), jnp.float32), 'Wout': n(ks[6], (D_MODEL, D_INNER))}

        def _mamba(x, Win, convw, convb, Wx, Wdt, bdt, Alog, Dp, Wout):
            B, L, _ = x.shape
            xz = jnp.einsum('bld,ed->ble', x, Win)
            u, z = jnp.split(xz, 2, axis=-1)
            uc = jnp.transpose(u, (0, 2, 1))
            uc = jnp.pad(uc, ((0, 0), (0, 0), (D_CONV - 1, 0)))
            uc = jax.lax.conv_general_dilated(uc, convw, (1,), 'VALID', feature_group_count=D_INNER)
            uc = uc + convb[None, :, None]
            u = jax.nn.silu(jnp.transpose(uc, (0, 2, 1)))
            xdbl = jnp.einsum('bld,ed->ble', u, Wx)
            dtr, Bm, Cm = jnp.split(xdbl, [DT_RANK, DT_RANK + D_STATE], axis=-1)
            dt = jax.nn.softplus(jnp.einsum('blr,dr->bld', dtr, Wdt) + bdt)
            A = -jnp.exp(Alog)

            def step(h, ins):
                dt_t, u_t, B_t, C_t = ins
                h = jnp.exp(dt_t[..., None] * A) * h + (dt_t * u_t)[..., None] * B_t[:, None, :]
                y_t = jnp.einsum('bdn,bn->bd', h, C_t)
                return (h, y_t)
            h0 = jnp.zeros((B, D_INNER, D_STATE), jnp.float32)
            xs = (jnp.moveaxis(dt, 1, 0), jnp.moveaxis(u, 1, 0), jnp.moveaxis(Bm, 1, 0), jnp.moveaxis(Cm, 1, 0))
            _, ys = jax.lax.scan(step, h0, xs)
            y = jnp.moveaxis(ys, 0, 1) + u * Dp
            y = y * jax.nn.silu(z)
            return jnp.einsum('bld,ed->ble', y, Wout)
        mu = jnp.mean(x, axis=-1, keepdims=True)
        var = jnp.var(x, axis=-1, keepdims=True)
        xn = (x - mu) * jax.lax.rsqrt(var + EPS) * norm_g + norm_b
        y_fwd = _mamba(xn, f_Win, f_convw, f_convb, f_Wx, f_Wdt, f_bdt, f_Alog, f_D, f_Wout)
        y_bwd = _mamba(jnp.flip(xn, axis=1), b_Win, b_convw, b_convb, b_Wx, b_Wdt, b_bdt, b_Alog, b_D, b_Wout)
        y_bwd = jnp.flip(y_bwd, axis=1)
        return x + y_fwd + y_bwd

    def _L0_ffn_ref(x, gate_w, ew1, ew2, ew3, sw1, sw2, sw3):
        import jax, jax.numpy as jnp
        import numpy as np
        EXPERTS = 8
        TOP_K = 2

        def swiglu(x, w1, w2, w3):
            h = x @ w1
            return h * jax.nn.sigmoid(h) * (x @ w2) @ w3
        B, S, D = x.shape
        gate_out = x @ gate_w
        top_v, top_i = jax.lax.top_k(gate_out, TOP_K)
        masked = jnp.full_like(gate_out, -1e+20)
        bi = jnp.arange(B)[:, None, None]
        si = jnp.arange(S)[None, :, None]
        masked = masked.at[bi, si, top_i].set(top_v)
        probs = jax.nn.softmax(masked, axis=-1)
        chosen = jnp.zeros_like(gate_out, dtype=bool).at[bi, si, top_i].set(True)
        w = jnp.where(chosen, probs, 0.0)

        def one_expert(w1, w2, w3, we):
            return swiglu(x, w1, w2, w3) * we[..., None]
        out = jax.vmap(one_expert, in_axes=(0, 0, 0, 2))(ew1, ew2, ew3, w).sum(0)
        out = out + swiglu(x, sw1, sw2, sw3)
        return out
    x = L0_attn_x
    mod = (_silu(L0_c) @ L0_wmod).reshape(L0_c.shape[0], 6, 1, -1)
    sa, ca, ga, sb, cb, gb = (mod[:, 0], mod[:, 1], mod[:, 2], mod[:, 3], mod[:, 4], mod[:, 5])
    ga = (2 * (ga >= 0) - 1) * jnp.maximum(jnp.abs(ga), 0.25)
    gb = (2 * (gb >= 0) - 1) * jnp.maximum(jnp.abs(gb), 0.25)
    h = _layernorm(x, axis=-1) * (1 + ca) + sa
    x = x + ga * _L0_attn_ref(h, L0_attn_norm_g, L0_attn_norm_b, L0_attn_f_Win, L0_attn_f_convw, L0_attn_f_convb, L0_attn_f_Wx, L0_attn_f_Wdt, L0_attn_f_bdt, L0_attn_f_Alog, L0_attn_f_D, L0_attn_f_Wout, L0_attn_b_Win, L0_attn_b_convw, L0_attn_b_convb, L0_attn_b_Wx, L0_attn_b_Wdt, L0_attn_b_bdt, L0_attn_b_Alog, L0_attn_b_D, L0_attn_b_Wout)
    h = _layernorm(x, axis=-1) * (1 + cb) + sb
    x = x + gb * _L0_ffn_ref(h, L0_ffn_gate_w, L0_ffn_ew1, L0_ffn_ew2, L0_ffn_ew3, L0_ffn_sw1, L0_ffn_sw2, L0_ffn_sw3)
    return x

_drawn_inputs = setup_inputs


def setup_inputs(seed=0):
    import zlib

    import numpy as np

    out = dict(_drawn_inputs(seed))
    spreads = {'L0_attn_norm_g': (1.0, 0.6),
     'L0_attn_norm_b': (0.0, 0.8),
     'L0_attn_f_D': (1.0, 0.6),
     'L0_attn_b_D': (1.0, 0.6)}
    factors = {'L0_attn_f_Win': 8.0,
     'L0_attn_f_convw': 8.0,
     'L0_attn_f_convb': 8.0,
     'L0_attn_f_Wx': 8.0,
     'L0_attn_f_bdt': 8.0,
     'L0_attn_f_Alog': 8.0,
     'L0_attn_f_Wout': 8.0,
     'L0_attn_b_Win': 8.0,
     'L0_attn_b_convw': 8.0,
     'L0_attn_b_convb': 8.0,
     'L0_attn_b_Wx': 8.0,
     'L0_attn_b_bdt': 8.0,
     'L0_attn_b_Alog': 8.0,
     'L0_attn_b_Wout': 8.0,
     'L0_ffn_gate_w': 8.0,
     'L0_ffn_ew1': 8.0,
     'L0_ffn_ew2': 8.0,
     'L0_ffn_ew3': 8.0,
     'L0_ffn_sw1': 8.0,
     'L0_ffn_sw2': 8.0,
     'L0_ffn_sw3': 8.0}
    for name, (base, spread) in spreads.items():
        noise = np.random.default_rng([zlib.crc32(name.encode()), seed]).standard_normal(out[name].shape)
        drawn = base * np.exp(spread * noise) if base else spread * noise
        out[name] = jnp.asarray(drawn.astype(out[name].dtype))
    for name, factor in factors.items():
        out[name] = (out[name] * factor).astype(out[name].dtype)
    return out
```

```python
import concourse.bass as bass
from concourse import mybir
from contextlib import ExitStack

NB, T, D = 16, 512, 128
P = 128
NT = T // P
E = 2 * D
NH = E // P
N = 16
R = 8
TAPS = 4
NX = 8
NE = NX + 1
HID = 2 * D
EPS = 1e-5
STEPS = 2 * N
PAD = TAPS - 1
KINDS = 6

XN = 0
U, DTR, BCP, DT, VT, Z = 0, 2, 3, 4, 6, 8
PREP = 10
POSTF = 1 + 2 * PREP
PIECES = POSTF + NH
POSTB, PROJ, H2T, GATE, DOWN = 0, 2, 3, 4, 5

PREP_B_SLOT, LN_SLOT, PREP_F_SLOT, POST_F_SLOT = 4, 17, 21, 17
FFN_UP_SLOT = 6


def piece(d, kind, half=0):
    return 1 + PREP * d + kind + half


def expert_slots():
    steps = []
    for e in range(NE):
        steps += [("up", e, 0), ("up", e, 1), ("down", e, 0)]
    at = {}
    for j, s in enumerate(steps):
        at.setdefault(min(FFN_UP_SLOT + j, STEPS - 1), []).append(s)
    return at


EXPERT_AT = expert_slots()
ORDER = [NX] + list(range(NX))


def adaln_mamba_moe(nc, t, out):
    f32, u32 = mybir.dt.float32, mybir.dt.uint32
    ALU, ACT = mybir.AluOpType, mybir.ActivationFunctionType
    ctx = ExitStack()
    with ctx:
        def sb(name, shape, dt=f32):
            return ctx.enter_context(nc.sbuf_tensor(name, shape, dt))

        def ps(name, shape):
            return ctx.enter_context(nc.psum_tensor(name, shape, f32))

        def sem(name):
            return ctx.enter_context(nc.semaphore(name))

        ident = sb("ident", [P, P])
        iota8 = sb("iota8", [P, NX])
        wdt_nat = [sb(f"wdt_nat{d}", [P, NH, R]) for d in range(2)]
        convw = [sb(f"convw{d}", [P, NH, TAPS]) for d in range(2)]
        convb = [sb(f"convb{d}", [P, NH]) for d in range(2)]
        bdt = [sb(f"bdt{d}", [P, NH]) for d in range(2)]
        skip = [sb(f"skip{d}", [P, NH]) for d in range(2)]
        alog = [sb(f"alog{d}", [P, NH, N]) for d in range(2)]
        aneg = [sb(f"aneg{d}", [P, NH, N]) for d in range(2)]
        wcT = [sb(f"wcT{d}", [D, NH, TAPS, P]) for d in range(2)]
        wzT = [sb(f"wzT{d}", [D, NH, P]) for d in range(2)]
        wxT = [sb(f"wxT{d}", [P, NH, R + 2 * N]) for d in range(2)]
        wdtT = [sb(f"wdtT{d}", [R, NH, P]) for d in range(2)]
        woutT = [sb(f"woutT{d}", [P, NH, D]) for d in range(2)]
        norm = sb("norm", [P, 2])
        gate_w = sb("gate_w", [D, NX])
        w1 = sb("w1", [D, NE, HID])
        w2 = sb("w2", [D, NE, HID])
        w3 = sb("w3", [P, NE, 2, D])
        c_nat = sb("c_nat", [NB, D])
        c_th = sb("c_th", [NB, D])
        c_silu = sb("c_silu", [NB, D])
        cT = sb("cT", [D, NB])
        gsgn = sb("gsgn", [NB, 2, D])
        gabs = sb("gabs", [NB, 2, D])
        modA = sb("modA", [P, 3, D])
        modF = sb("modF", [P, 4, D])
        x = sb("x", [P, NT, D])
        st = sb("st", [P, NT, 6])
        stat = sb("stat", [P, NT, 6])
        mhalf = sb("mhalf", [P, NT])
        rstd = sb("rstd", [P, NT])
        z1 = sb("z1", [P, NT, D])
        h1m = sb("h1m", [P, NT, D])
        h1 = sb("h1", [P, NT, D])
        xn = sb("xn", [P, NT, D])
        xnT = sb("xnT", [D, T + 2 * PAD])
        rt = sb("rt", [P, NT, D])
        rN = sb("rN", [P, NT, D])
        rC = sb("rC", [P, NT, D])
        xh = sb("xh", [P, T])
        th = sb("th", [P, T])
        u = [sb(f"u{d}", [P, NH, T]) for d in range(2)]
        zs = [sb(f"zs{d}", [P, NH, T]) for d in range(2)]
        dtr = sb("dtr", [R, T])
        bc = [sb(f"bc{d}", [P, NT, 2 * N]) for d in range(2)]
        xb = sb("xb", [P, NH, T])
        ab = sb("ab", [P, NH, T])
        dt_ = [sb(f"dt{d}", [P, NH, T]) for d in range(2)]
        v = sb("v", [P, NH, T])
        vT = [sb(f"vT{d}", [P, NT, E]) for d in range(2)]
        bt = sb("bt", [P, 2, NT, E])
        a = [sb(f"a{d}", [P, 2, NH, T]) for d in range(2)]
        h = sb("h", [P, 2, NH, T])
        acc = [sb(f"acc{d}", [P, NT, E]) for d in range(2)]
        def part(buf, rows, lo, shape):
            flat = buf.rearrange("p a b c -> p (a b c)") if len(buf.shape) == 4 else buf.rearrange("p a b -> p (a b)")
            size = 1
            for k in shape:
                size *= k
            flat = flat[0:rows, lo:lo + size]
            if len(shape) == 1:
                return flat
            if len(shape) == 2:
                return flat.rearrange("p (a b) -> p a b", b=shape[1])
            return flat.rearrange("p (a b c) -> p a b c", b=shape[1], c=shape[2])

        win_tap = [part(bt[:, :, :, :], P, d * NH * TAPS * D, [NH, TAPS, D]) for d in range(2)]
        win_nat = [part(h[:, :, :, :], P, d * 4 * D, [4, D]) for d in range(2)]
        wx_nat = [part(h[:, :, :, :], R + 2 * N, 8 * D + d * E, [E]) for d in range(2)]
        wout_nat = [part(h[:, :, :, :], D, 12 * D + d * E, [E]) for d in range(2)]
        wmod = part(acc[0][:, :, :], D, 0, [KINDS * D])
        mod = part(acc[1][:, :, :], NB, 0, [KINDS, D])
        yt = [sb(f"yt{d}", [P, T]) for d in range(2)]
        yg = [sb(f"yg{d}", [P, NH, T]) for d in range(2)]
        fx = sb("fx", [P, NT, D])
        x2 = sb("x2", [P, NT, D])
        stF = sb("stF", [P, NT, 6])
        statF = sb("statF", [P, NT, 6])
        rstdF = sb("rstdF", [P, NT])
        zF = sb("zF", [P, NT, D])
        h2m = sb("h2m", [P, NT, D])
        h2 = sb("h2", [P, NT, D])
        h2T = sb("h2T", [D, T])
        gl = sb("gl", [P, NT, NX])
        gl2 = sb("gl2", [P, NT, NX])
        top = sb("top", [P, NT, NX])
        topi = sb("topi", [P, NT, NX], u32)
        topf = sb("topf", [P, NT, 2])
        gd = sb("gd", [P, NT])
        ge = sb("ge", [P, NT])
        gs = sb("gs", [P, NT])
        gw = sb("gw", [P, 2, NT])
        hot = sb("hot", [P, 2, NT, NX])
        hotw = sb("hotw", [P, 2, NT, NX])
        wts = sb("wts", [P, NT, NX])
        tf = sb("tf", [P, T])
        pf = sb("pf", [P, T])
        act = sb("act", [P, 2, T])
        facc = sb("facc", [P, NT, D])
        fo = sb("fo", [P, NT, D])
        osb = sb("osb", [P, NT, D])

        psB = ps("psB", [P, NH * T])
        psH = ps("psH", [P, NT * E])
        psP = ps("psP", [P, T])
        F0 = ps("F0", [P, T])
        F1 = ps("F1", [P, T])
        F2 = ps("F2", [P, T])

        mod_dram = nc.dram_tensor("mod_table", (NB, KINDS * D), f32, kind="Internal").ap()

        loaded = sem("loaded")
        const_ok = sem("const_ok")
        ident_ok = sem("ident_ok")
        taps_ok = sem("taps_ok")
        wt_tr = sem("wt_tr")
        wt_ev = sem("wt_ev")
        halved = sem("halved")
        c_step = sem("c_step")
        mod_mm = sem("mod_mm")
        mod_v = sem("mod_v")
        mod_out = sem("mod_out")
        x_in = sem("x_in")
        modA_in = sem("modA_in")
        lnA = sem("lnA")
        rstdA = sem("rstdA")
        zA = sem("zA")
        h1_s = sem("h1_s")
        rN_s = sem("rN_s")
        rC_s = sem("rC_s")
        pP_full = sem("pP_full")
        pP_free = sem("pP_free")
        th_s = sem("th_s")
        silu_s = sem("silu_s")
        sp_s = sem("sp_s")
        dt_s = sem("dt_s")
        v_s = sem("v_s")
        bt_s = sem("bt_s")
        pB_full = sem("pB_full")
        a_s = sem("a_s")
        h_s = sem("h_s")
        pH_full = sem("pH_full")
        acc_s = sem("acc_s")
        yg_s = [sem("yg_f_s"), sem("yg_b_s")]
        modF_in = sem("modF_in")
        F2_full = sem("F2_full")
        F2_free = sem("F2_free")
        x2_s = sem("x2_s")
        lnF = sem("lnF")
        rstdF_s = sem("rstdF_s")
        zF_s = sem("zF_s")
        h2_s = sem("h2_s")
        gate_s = sem("gate_s")
        ge_s = sem("ge_s")
        F0_full = sem("F0_full")
        F1_full = sem("F1_full")
        tf_s = sem("tf_s")
        pf_s = sem("pf_s")
        act_s = sem("act_s")
        facc_s = sem("facc_s")
        gw_s = sem("gw_s")
        o_s = sem("o_s")
        out_d = sem("out_d")
        GATES = 13
        GATE_D = 6
        LOADS = 16 * 29
        MOD_STEPS = 12
        CONSTS = 8

        block = ctx.enter_context(nc.Block())

        def wait(eng, s, value):
            if not (isinstance(value, int) and value <= 0):
                eng.wait_ge(s, value)

        def passes(eng, body):
            body(0, True, False, False)
            body(1, True, True, False)
            with eng.Fori(2, NB - 1) as b:
                body(b, True, True, False)
            body(NB - 1, True, True, True)
            body(NB, False, True, True)

        @block.sync
        def _(sp):
            small = nc.allow_non_contiguous_dma(reason="small weight columns")
            with small:
                for d in range(2):
                    w = t["fb"[d]]
                    for dst, src in (
                        (win_nat[d][:, :, :], w["Win"].rearrange("(k p) d -> p k d", p=P)),
                        (wx_nat[d][:, :], w["Wx"]),
                        (wdt_nat[d][:, :, :], w["Wdt"].rearrange("(k p) r -> p k r", p=P)),
                        (wout_nat[d][:, :], w["Wout"]),
                        (convw[d][:, :, :], w["convw"].rearrange("(k p) a j -> p k (a j)", p=P)),
                        (convb[d][:, :], w["convb"].rearrange("(k p) -> p k", p=P)),
                        (bdt[d][:, :], w["bdt"].rearrange("(k p) -> p k", p=P)),
                        (skip[d][:, :], w["D"].rearrange("(k p) -> p k", p=P)),
                        (alog[d][:, :, :], w["Alog"].rearrange("(k p) n -> p k n", p=P)),
                        (norm[:, d:d + 1], t["norm_g" if d == 0 else "norm_b"].rearrange("(p a) -> p a", a=1)),
                    ):
                        sp.dma_start(dst, src).then_inc(loaded, 16)
                for dst, src in (
                    (c_nat[:, :], t["c"]),
                    (wmod[:, :], t["wmod"]),
                    (gate_w[:, :], t["gate_w"]),
                    (w1[:, 0:NX, :], t["ew1"].rearrange("e d h -> d e h")),
                    (w2[:, 0:NX, :], t["ew2"].rearrange("e d h -> d e h")),
                    (w3[:, 0:NX, :, :], t["ew3"].rearrange("e (k p) d -> p e k d", p=P)),
                    (w1[:, NX, :], t["sw1"]),
                    (w2[:, NX, :], t["sw2"]),
                    (w3[:, NX, :, :], t["sw3"].rearrange("(k p) d -> p k d", p=P)),
                ):
                    sp.dma_start(dst, src).then_inc(loaded, 16)
            sp.wait_ge(mod_v, MOD_STEPS)
            sp.dma_start(mod_dram, mod[:, :, :].rearrange("b k d -> b (k d)")).then_inc(mod_out, 16)
            sp.wait_ge(mod_out, 16)

            def load(b):
                wait(sp, rN_s, 2 * b)
                sp.dma_start(x[:, :, :], t["x"][bass.ds(b, 1)].rearrange("a (k p) d -> p (a k) d", p=P))\
                    .then_inc(x_in, 16)
                row = mod_dram[bass.ds(b, 1), 0:3 * D].broadcast_to([P, 3 * D])
                sp.dma_start(modA[:, :, :].rearrange("p k d -> p (k d)"), row).then_inc(modA_in, 16)

            load(0)

            def body(b, scan, ffn, last):
                if ffn:
                    fb = b - 1
                    wait(sp, o_s, 2 * fb)
                    row = mod_dram[bass.ds(fb, 1), 2 * D:6 * D].broadcast_to([P, 4 * D])
                    sp.dma_start(modF[:, :, :].rearrange("p k d -> p (k d)"), row).then_inc(modF_in, 16)
                if scan and not last:
                    load(b + 1)
                if ffn:
                    sp.wait_ge(o_s, 2 * fb + 2)
                    sp.dma_start(out[bass.ds(fb, 1)].rearrange("a (k p) d -> p (a k) d", p=P), osb[:, :, :])\
                        .then_inc(out_d, 16)

            passes(sp, body)
            sp.wait_ge(out_d, 16 * NB)

        @block.gpsimd
        def _(pool):
            g = nc.gpsimd
            g.memset(ident[:, :], 0.0).then_inc(ident_ok, 1)
            pool.wait_ge(ident_ok, 1)
            g.affine_select(out=ident[:, :], in_=ident[:, :], compare_op=ALU.not_equal, fill=1.0, base=0,
                            pattern=[[-1, P]], channel_multiplier=1).then_inc(ident_ok, 1)
            g.iota(iota8[:, :], pattern=[[1, NX]], base=0, channel_multiplier=0,
                   allow_small_or_imprecise_dtypes=True).then_inc(const_ok, 1)
            g.memset(mhalf[:, :], -0.5).then_inc(const_ok, 1)

            def over_tiles(row):
                return row.unsqueeze(1).broadcast_to([P, NT, D])

            def bmul(step, d, n):
                wait(pool, pB_full, step - 1)
                if n == 0:
                    wait(pool, pP_free, PIECES * bmul.b + piece(d, VT, 1) + 1)
                g.tensor_tensor(bt[:, n % 2, :, :], vT[d][:, :, :],
                                bc[d][:, :, n:n + 1].broadcast_to([P, NT, E]), ALU.mult).then_inc(bt_s, 1)

            def rsqrt(dst, src):
                return g.tensor_tensor(dst, src, mhalf[:, :], ALU.pow)

            def norms(b, slot):
                if slot == LN_SLOT:
                    if isinstance(b, int) and b == 0:
                        pool.wait_ge(const_ok, CONSTS)
                    pool.wait_ge(lnA, 20 * b + 10)
                    rsqrt(rstd[:, :], stat[:, :, 3]).then_inc(rstdA, 1)
                    pool.wait_ge(zA, 8 * b + 4)
                    pool.wait_ge(modA_in, 16 * b + 16)
                    g.tensor_tensor(h1m[:, :, :], z1[:, :, :], over_tiles(modA[:, 1, :]), ALU.mult).then_inc(h1_s, 1)
                    pool.wait_ge(h1_s, 2 * b + 1)
                    g.tensor_tensor(h1[:, :, :], h1m[:, :, :], over_tiles(modA[:, 0, :]), ALU.add).then_inc(h1_s, 1)
                if slot == LN_SLOT + 1:
                    pool.wait_ge(lnA, 20 * b + 20)
                    rsqrt(rstd[:, :], stat[:, :, 3]).then_inc(rstdA, 1)
                if slot == LN_SLOT + 3:
                    pool.wait_ge(h1_s, 2 * b + 2)
                    g.tensor_tensor(rt[:, :, :], h1[:, :, :], over_tiles(modA[:, 2, :]), ALU.mult).then_inc(rN_s, 1)
                    pool.wait_ge(rN_s, 2 * b + 1)
                    wait(pool, rC_s, b)
                    pool.wait_ge(x_in, 16 * b + 16)
                    g.tensor_tensor(rN[:, :, :], rt[:, :, :], x[:, :, :], ALU.add).then_inc(rN_s, 1)

            def make_v(b, d):
                pool.wait_ge(dt_s, 2 * b + d + 1)
                wait(pool, pP_full, PIECES * (b - 1) + piece(1, VT, 1) + 1 if d == 0
                     else PIECES * b + piece(0, VT, 1) + 1)
                g.tensor_tensor(v[:, :, :], u[d][:, :, :], dt_[d][:, :, :], ALU.mult).then_inc(v_s, 1)

            def gate_y(b, d, half):
                if d == 0:
                    pool.wait_ge(pP_free, PIECES * b + POSTF + half + 1)
                    wait(pool, F2_full, (DOWN + NE) * (b - 1) + PROJ + 1)
                else:
                    pool.wait_ge(F2_free, (DOWN + 1) * b + POSTB + half + 1)
                g.tensor_tensor(yg[d][:, half, :], yt[d][:, :], zs[d][:, half, :], ALU.mult).then_inc(yg_s[d], 1)

            def ffn_side(fb, slot):
                if slot in (1, 2):
                    gate_y(fb, 1, slot - 1)
                if slot == 3:
                    pool.wait_ge(F2_free, (DOWN + 1) * fb + PROJ + 1)
                    pool.wait_ge(rC_s, fb + 1)
                    wait(pool, o_s, 2 * fb)
                    g.tensor_tensor(x2[:, :, :], fx[:, :, :], rC[:, :, :], ALU.add).then_inc(x2_s, 1)
                if slot == 4:
                    pool.wait_ge(lnF, 10 * fb + 10)
                    rsqrt(rstdF[:, :], statF[:, :, 3]).then_inc(rstdF_s, 1)
                    pool.wait_ge(zF_s, NT * fb + NT)
                    g.tensor_tensor(h2m[:, :, :], zF[:, :, :], over_tiles(modF[:, 2, :]), ALU.mult).then_inc(h2_s, 1)
                    pool.wait_ge(h2_s, 2 * fb + 1)
                    wait(pool, F2_full, (DOWN + NE) * fb)
                    g.tensor_tensor(h2[:, :, :], h2m[:, :, :], over_tiles(modF[:, 1, :]), ALU.add).then_inc(h2_s, 1)
                if slot == STEPS - 1:
                    pool.wait_ge(facc_s, NX * NT * fb + NX * NT)
                    g.tensor_tensor(fo[:, :, :], facc[:, :, :], over_tiles(modF[:, 3, :]), ALU.mult).then_inc(o_s, 1)
                    pool.wait_ge(o_s, 2 * fb + 1)
                    wait(pool, out_d, 16 * fb)
                    g.tensor_tensor(osb[:, :, :], fo[:, :, :], x2[:, :, :], ALU.add).then_inc(o_s, 1)

            def side(b, slot, prep_b, prep_f, post_f):
                if post_f and slot in (POST_F_SLOT, POST_F_SLOT + 1):
                    gate_y(b, 0, slot - POST_F_SLOT)
                if prep_f is not None:
                    norms(prep_f, slot)
                    if slot == PREP_F_SLOT + 5:
                        make_v(prep_f, 0)
                if prep_b and slot == PREP_B_SLOT + 5:
                    make_v(b, 1)

            for slot in range(STEPS):
                side(-1, slot, False, 0, False)
            bmul.b = 0
            bmul(0, 0, 0)

            def body(b, scan, ffn, last):
                for slot in range(STEPS):
                    if scan:
                        nxt = slot + 1
                        if nxt < STEPS:
                            bmul.b = b
                            bmul(STEPS * b + nxt, nxt // N, nxt % N)
                        elif not last:
                            bmul.b = b + 1
                            bmul(STEPS * b + nxt, 0, 0)
                    if scan:
                        side(b, slot, True, None if last else b + 1, True)
                    if ffn:
                        ffn_side(b - 1, slot)

            passes(pool, body)

        @block.scalar
        def _(act_e):
            s = nc.scalar
            act_e.wait_ge(loaded, LOADS)
            s.activation(c_th[:, :], c_nat[:, :], ACT.Tanh, scale=0.5).then_inc(c_step, 1)
            for d in range(2):
                s.activation(aneg[d][:, :, :], alog[d][:, :, :], ACT.Exp).then_inc(halved, 1)
            act_e.wait_ge(halved, 2)
            for d in range(2):
                s.activation(aneg[d][:, :, :], aneg[d][:, :, :], ACT.Copy, scale=-1.0).then_inc(halved, 1)
                s.activation(convb[d][:, :], convb[d][:, :], ACT.Copy, scale=0.5).then_inc(halved, 1)
            s.activation(w3[:, :, :, :], w3[:, :, :, :], ACT.Copy, scale=0.5).then_inc(halved, 1)
            for d in range(2):
                act_e.wait_ge(wt_tr, d + 1)
                s.activation(wcT[d][:, :, :, :], psB[:, 0:NH * TAPS * P], ACT.Copy).then_inc(wt_ev, 1)
                s.activation(wzT[d][:, :, :], psH[:, 0:NH * P], ACT.Copy).then_inc(wt_ev, 1)
                s.activation(wxT[d][:, :, :], psH[:, 2 * P:4 * P].rearrange("p (k c) -> p k c", c=P)[:, :, 0:R + 2 * N],
                             ACT.Copy).then_inc(wt_ev, 1)
                s.activation(wdtT[d][:, :, :], psH[0:R, 4 * P:6 * P], ACT.Copy).then_inc(wt_ev, 1)
                s.activation(woutT[d][:, :, :], psH[:, 6 * P:8 * P], ACT.Copy).then_inc(wt_ev, 1)
            act_e.wait_ge(c_step, 3)
            s.activation(cT[:, :], F0[:, 0:NB], ACT.Copy).then_inc(c_step, 1)
            act_e.wait_ge(halved, 7)

            def exps(step, b, d, n):
                wait(act_e, h_s, step - 1)
                if n == 0:
                    act_e.wait_ge(dt_s, 2 * b + d + 1)
                lo, hi = (1, T) if d == 0 else (0, T - 1)
                for half in range(NH):
                    s.activation(a[d][:, n % 2, half, lo:hi], dt_[d][:, half, lo:hi], ACT.Exp,
                                 scale=aneg[d][:, half, n:n + 1]).then_inc(a_s, 1)

            def take(b, pos):
                act_e.wait_ge(pP_full, PIECES * b + pos + 1)

            def silu(b, d, kind, half):
                k = 8 * b + 4 * d + (0 if kind == U else 2) + half
                take(b, piece(d, kind, half))
                wait(act_e, silu_s, k)
                if kind == U:
                    s.activation(xh[:, :], psP[:, :], ACT.Identity, scale=0.5,
                                 bias=convb[d][:, half:half + 1]).then_inc(pP_free, 1)
                else:
                    s.activation(xh[:, :], psP[:, :], ACT.Copy, scale=0.5).then_inc(pP_free, 1)
                act_e.wait_ge(pP_free, PIECES * b + piece(d, kind, half) + 1)
                s.activation(th[:, :], xh[:, :], ACT.Tanh).then_inc(th_s, 1)

            def prep(b, d, k):
                if k in (0, 1):
                    silu(b, d, U, k)
                if k == 2:
                    take(b, piece(d, DTR))
                    s.activation(dtr[:, :], psP[0:R, :], ACT.Copy).then_inc(pP_free, 1)
                    take(b, piece(d, BCP))
                    s.activation(bc[d][:, :, :], psP[:, 0:NT * 2 * N], ACT.Copy).then_inc(pP_free, 1)
                if k in (3, 4):
                    half = k - 3
                    q = 5 * (2 * b + d)
                    take(b, piece(d, DT, half))
                    wait(act_e, dt_s, 2 * b + d)
                    s.activation(xb[:, half, :], psP[:, :], ACT.Identity,
                                 bias=bdt[d][:, half:half + 1]).then_inc(pP_free, 1)
                    act_e.wait_ge(pP_free, PIECES * b + piece(d, DT, half) + 1)
                    s.activation(ab[:, half, :], xb[:, half, :], ACT.Abs).then_inc(sp_s, 1)
                    act_e.wait_ge(sp_s, q + 2 * half + 1)
                    s.activation(ab[:, half, :], ab[:, half, :], ACT.Exp, scale=-1.0).then_inc(sp_s, 1)
                    if half == 1:
                        act_e.wait_ge(sp_s, q + 4)
                        s.activation(ab[:, :, :], ab[:, :, :], ACT.Ln, bias=1.0).then_inc(sp_s, 1)
                if k in (6, 7):
                    half = k - 6
                    take(b, piece(d, VT, half))
                    s.activation(vT[d][:, :, half * P:half * P + P], psP[:, :].rearrange("p (k c) -> p k c", c=P),
                                 ACT.Copy).then_inc(pP_free, 1)
                if k in (8, 9):
                    silu(b, d, Z, k - 8)

            def side(b, slot, prep_b, prep_f):
                if prep_f is not None:
                    if slot == LN_SLOT + 3:
                        take(prep_f, XN)
                        s.activation(xnT[:, PAD:PAD + T], psP[:, :], ACT.Identity, scale=norm[:, 0:1],
                                     bias=norm[:, 1:2]).then_inc(pP_free, 1)
                    prep(prep_f, 0, slot - PREP_F_SLOT)
                if prep_b:
                    prep(b, 1, slot - PREP_B_SLOT)

            def ffn_side(fb, slot):
                if slot == 5:
                    act_e.wait_ge(F2_full, (DOWN + NE) * fb + H2T + 1)
                    s.activation(h2T[:, :], F2[:, :], ACT.Copy).then_inc(F2_free, 1)
                if slot == 7:
                    act_e.wait_ge(gate_s, GATES * fb + GATE_D)
                    s.activation(ge[:, :], gd[:, :], ACT.Exp).then_inc(ge_s, 1)
                for kind, e, half in EXPERT_AT.get(slot, ()):
                    k = 2 * NE * fb + 2 * e + half
                    if kind == "up":
                        act_e.wait_ge(F0_full, k + 1)
                        wait(act_e, pf_s, k)
                        s.activation(tf[:, :], F0[:, :], ACT.Tanh, scale=0.5).then_inc(tf_s, 1)
                    elif e == 0:
                        act_e.wait_ge(F2_full, (DOWN + NE) * fb + DOWN + 1)
                        wait(act_e, o_s, 2 * fb)
                        s.activation(facc[:, :, :], F2[:, :], ACT.Copy).then_inc(F2_free, 1)

            for slot in range(STEPS):
                side(-1, slot, False, 0)
            act_e.wait_ge(const_ok, CONSTS)
            exps(0, 0, 0, 0)

            def body(b, scan, ffn, last):
                for slot in range(STEPS):
                    nxt = slot + 1
                    if scan and nxt < STEPS:
                        exps(STEPS * b + nxt, b, nxt // N, nxt % N)
                    elif scan and not last:
                        exps(STEPS * b + nxt, b + 1, 0, 0)
                    if scan:
                        if slot == 4:
                            wait(act_e, x2_s, b)
                            act_e.wait_ge(rN_s, 2 * b + 2)
                            s.activation(rC[:, :, :], rN[:, :, :], ACT.Copy).then_inc(rC_s, 1)
                        side(b, slot, True, None if last else b + 1)
                    if ffn:
                        ffn_side(b - 1, slot)

            passes(act_e, body)

        @block.vector
        def _(dve):
            w = nc.vector
            w.memset(xnT[:, 0:PAD], 0.0).then_inc(const_ok, 1)
            w.memset(xnT[:, PAD + T:], 0.0).then_inc(const_ok, 1)
            for ring in range(2):
                w.memset(a[0][:, ring, :, 0:1], 0.0).then_inc(const_ok, 1)
                w.memset(a[1][:, ring, :, T - 1:T], 0.0).then_inc(const_ok, 1)
            dve.wait_ge(loaded, LOADS)
            for d in range(2):
                for half in range(NH):
                    for j in range(TAPS):
                        w.tensor_scalar(win_tap[d][:, half, j, :], win_nat[d][:, half, :],
                                        convw[d][:, half, j:j + 1], None, ALU.mult).then_inc(taps_ok, 1)
            dve.wait_ge(c_step, 1)
            w.scalar_tensor_tensor(c_silu[:, :], c_th[:, :], 1.0, c_nat[:, :], ALU.add, ALU.mult).then_inc(c_step, 1)
            dve.wait_ge(mod_mm, 1)
            for k in range(KINDS):
                src = (F0, F1)[k // 4][0:NB, (k % 4) * D:(k % 4) * D + D]
                w.tensor_scalar(mod[:, k, :], src, 0.5, 1.0 if k % 3 == 1 else 0.0, ALU.mult, ALU.add)\
                    .then_inc(mod_v, 1)
            dve.wait_ge(mod_v, KINDS)
            gates = mod[:, 2:6:3, :]
            w.tensor_scalar(gsgn[:, :, :], gates, 0.0, 2.0, ALU.is_ge, ALU.mult).then_inc(mod_v, 1)
            w.scalar_tensor_tensor(gabs[:, :, :], gates, -1.0, gates, ALU.mult, ALU.max).then_inc(mod_v, 1)
            dve.wait_ge(mod_v, KINDS + 2)
            w.tensor_scalar(gabs[:, :, :], gabs[:, :, :], 0.25, None, ALU.max).then_inc(mod_v, 1)
            w.tensor_scalar(gsgn[:, :, :], gsgn[:, :, :], -1.0, None, ALU.add).then_inc(mod_v, 1)
            dve.wait_ge(mod_v, KINDS + 4)
            for k in range(2):
                w.tensor_tensor(mod[:, 2 + 3 * k, :], gsgn[:, k, :], gabs[:, k, :], ALU.mult).then_inc(mod_v, 1)
            dve.wait_ge(mod_v, MOD_STEPS)

            def scan(step, d, n):
                dve.wait_ge(pB_full, step + 1)
                dve.wait_ge(a_s, NH * (step + 1))
                wait(dve, pH_full, step - 1)
                order = slice(None) if d == 0 else slice(None, None, -1)
                w.tensor_tensor_scan(h[:, n % 2, :, :].rearrange("p k t -> p (k t)")[:, order],
                                     a[d][:, n % 2, :, :].rearrange("p k t -> p (k t)")[:, order],
                                     psB[:, order], 0.0, ALU.mult, ALU.add).then_inc(h_s, 1)

            def read_out(step, d, n, b):
                dve.wait_ge(pH_full, step + 1)
                wait(dve, acc_s, NT * step)
                if n == 0:
                    if d == 0:
                        wait(dve, pP_full, PIECES * (b - 1) + POSTF + NH)
                    else:
                        wait(dve, F2_full, (DOWN + NE) * (b - 1) + POSTB + NH)
                for i in range(NT):
                    dst, src = acc[d][:, i, :], psH[:, i * E:i * E + E]
                    c = bc[d][:, i, N + n:N + n + 1]
                    if n == 0:
                        w.tensor_scalar(dst, src, c, None, ALU.mult).then_inc(acc_s, 1)
                    else:
                        w.scalar_tensor_tensor(dst, src, c, dst, ALU.mult, ALU.add).then_inc(acc_s, 1)

            def statistics(x_, st_, stat_, sig, q):
                for i in range(NT):
                    w.bn_stats(st_[:, i, :], x_[:, i, :]).then_inc(sig, 1)
                dve.wait_ge(sig, q + 4)
                w.tensor_tensor(stat_[:, :, 0:2], st_[:, :, 1:3], st_[:, :, 4:6], ALU.add).then_inc(sig, 1)
                w.tensor_tensor(stat_[:, :, 4:5], st_[:, :, 1:2], st_[:, :, 4:5], ALU.subtract).then_inc(sig, 1)
                dve.wait_ge(sig, q + 6)
                w.tensor_scalar(stat_[:, :, 2:3], stat_[:, :, 0:1], 0.5, None, ALU.mult).then_inc(sig, 1)
                w.scalar_tensor_tensor(stat_[:, :, 5:6], stat_[:, :, 4:5], D / 4.0, stat_[:, :, 4:5],
                                       ALU.mult, ALU.mult).then_inc(sig, 1)
                dve.wait_ge(sig, q + 8)
                w.tensor_tensor(stat_[:, :, 1:2], stat_[:, :, 1:2], stat_[:, :, 5:6], ALU.add).then_inc(sig, 1)
                dve.wait_ge(sig, q + 9)
                w.tensor_scalar(stat_[:, :, 3:4], stat_[:, :, 1:2], 1.0 / D, EPS, ALU.mult, ALU.add).then_inc(sig, 1)

            def normalize(dst, x_, stat_, rstd_, sig):
                for i in range(NT):
                    w.tensor_scalar(dst[:, i, :], x_[:, i, :], stat_[:, i, 2:3], rstd_[:, i:i + 1],
                                    ALU.subtract, ALU.mult).then_inc(sig, 1)

            def norms(b, slot):
                if slot == LN_SLOT:
                    dve.wait_ge(x_in, 16 * b + 16)
                    wait(dve, zA, 8 * b)
                    statistics(x, st, stat, lnA, 20 * b)
                    dve.wait_ge(rstdA, 2 * b + 1)
                    wait(dve, h1_s, 2 * b)
                    normalize(z1, x, stat, rstd, zA)
                if slot == LN_SLOT + 1:
                    dve.wait_ge(h1_s, 2 * b + 2)
                    dve.wait_ge(zA, 8 * b + 4)
                    statistics(h1, st, stat, lnA, 20 * b + 10)
                if slot == LN_SLOT + 2:
                    dve.wait_ge(rstdA, 2 * b + 2)
                    wait(dve, pP_full, PIECES * (b - 1) + XN + 1)
                    normalize(xn, h1, stat, rstd, zA)

            def silu(b, d, kind, half):
                k = 8 * b + 4 * d + (0 if kind == U else 2) + half
                dve.wait_ge(th_s, k + 1)
                wait(dve, yg_s[d], NH * b)
                dst = (u if kind == U else zs)[d][:, half, :]
                w.scalar_tensor_tensor(dst, th[:, :], 1.0, xh[:, :], ALU.add, ALU.mult).then_inc(silu_s, 1)

            def prep(b, d, k):
                if k in (0, 1):
                    silu(b, d, U, k)
                if k == 4:
                    dve.wait_ge(sp_s, 5 * (2 * b + d) + 5)
                    w.scalar_tensor_tensor(dt_[d][:, :, :], xb[:, :, :], 0.0, ab[:, :, :], ALU.max, ALU.add)\
                        .then_inc(dt_s, 1)
                if k in (8, 9):
                    silu(b, d, Z, k - 8)

            def skip_add(b, d, half):
                if d == 0:
                    dve.wait_ge(pP_full, PIECES * b + POSTF + half + 1)
                    src, sig = psP, pP_free
                else:
                    dve.wait_ge(F2_full, (DOWN + NE) * b + POSTB + half + 1)
                    src, sig = F2, F2_free
                wait(dve, yg_s[d], NH * b + half)
                w.scalar_tensor_tensor(yt[d][:, :], u[d][:, half, :], skip[d][:, half:half + 1], src[:, :],
                                       ALU.mult, ALU.add).then_inc(sig, 1)

            def gate(fb):
                q = GATES * fb
                dve.wait_ge(F2_full, (DOWN + NE) * fb + GATE + 1)
                w.tensor_copy(gl[:, :, :], F2[:, 0:NT * NX]).then_inc(F2_free, 1)
                dve.wait_ge(F2_free, (DOWN + 1) * fb + GATE + 1)
                w.tensor_copy(gl2[:, :, :], gl[:, :, :]).then_inc(gate_s, 1)
                for i in range(NT):
                    w.max(top[:, i, :], gl[:, i, :]).then_inc(gate_s, 1)
                dve.wait_ge(gate_s, q + 5)
                w.tensor_tensor(gd[:, :], top[:, :, 1], top[:, :, 0], ALU.subtract).then_inc(gate_s, 1)
                for i in range(NT):
                    w.max_index(topi[:, i, :], top[:, i, :], gl2[:, i, :]).then_inc(gate_s, 1)
                dve.wait_ge(gate_s, q + 10)
                w.tensor_copy(topf[:, :, :], topi[:, :, 0:2]).then_inc(gate_s, 1)
                dve.wait_ge(gate_s, q + 11)
                for j in range(2):
                    w.tensor_tensor(hot[:, j, :, :], iota8[:, :].unsqueeze(1).broadcast_to([P, NT, NX]),
                                    topf[:, :, j:j + 1].broadcast_to([P, NT, NX]), ALU.is_equal).then_inc(gate_s, 1)

            def gate_weights(fb):
                q = 6 * fb
                dve.wait_ge(ge_s, fb + 1)
                w.tensor_scalar(gs[:, :], ge[:, :], 1.0, None, ALU.add).then_inc(gw_s, 1)
                dve.wait_ge(gw_s, q + 1)
                w.reciprocal(gw[:, 0, :], gs[:, :]).then_inc(gw_s, 1)
                dve.wait_ge(gw_s, q + 2)
                w.tensor_tensor(gw[:, 1, :], gw[:, 0, :], ge[:, :], ALU.mult).then_inc(gw_s, 1)
                dve.wait_ge(gate_s, GATES * fb + GATES)
                dve.wait_ge(gw_s, q + 3)
                for j in range(2):
                    w.tensor_tensor(hotw[:, j, :, :], hot[:, j, :, :],
                                    gw[:, j, :].unsqueeze(2).broadcast_to([P, NT, NX]), ALU.mult).then_inc(gw_s, 1)
                dve.wait_ge(gw_s, q + 5)
                wait(dve, facc_s, NX * NT * fb)
                w.tensor_tensor(wts[:, :, :], hotw[:, 0, :, :], hotw[:, 1, :, :], ALU.add).then_inc(gw_s, 1)

            def ffn_side(fb, slot):
                if slot in (1, 2):
                    skip_add(fb, 1, slot - 1)
                if slot == 3:
                    dve.wait_ge(F2_full, (DOWN + NE) * fb + PROJ + 1)
                    dve.wait_ge(modF_in, 16 * fb + 16)
                    wait(dve, x2_s, fb)
                    w.tensor_tensor(fx[:, :, :], F2[:, :].rearrange("p (k c) -> p k c", c=D),
                                    modF[:, 0, :].unsqueeze(1).broadcast_to([P, NT, D]), ALU.mult).then_inc(F2_free, 1)
                if slot == 4:
                    dve.wait_ge(x2_s, fb + 1)
                    wait(dve, zF_s, NT * fb)
                    statistics(x2, stF, statF, lnF, 10 * fb)
                    dve.wait_ge(rstdF_s, fb + 1)
                    wait(dve, h2_s, 2 * fb)
                    normalize(zF, x2, statF, rstdF, zF_s)
                if slot == 6:
                    gate(fb)
                if slot == 8:
                    gate_weights(fb)
                for kind, e, half in EXPERT_AT.get(slot, ()):
                    k = 2 * NE * fb + 2 * e + half
                    if kind == "up":
                        dve.wait_ge(tf_s, k + 1)
                        wait(dve, act_s, k)
                        w.scalar_tensor_tensor(pf[:, :], tf[:, :], 1.0, F0[:, :], ALU.add, ALU.mult).then_inc(pf_s, 1)
                        dve.wait_ge(pf_s, k + 1)
                        dve.wait_ge(F1_full, k + 1)
                        wait(dve, F2_full, (DOWN + NE) * fb + DOWN + e if e else (DOWN + NE) * fb)
                        w.tensor_tensor(act[:, half, :], pf[:, :], F1[:, :], ALU.mult).then_inc(act_s, 1)
                    elif e > 0:
                        dve.wait_ge(F2_full, (DOWN + NE) * fb + DOWN + e + 1)
                        if e == 1:
                            dve.wait_ge(F2_free, (DOWN + 1) * fb + DOWN + 1)
                            dve.wait_ge(gw_s, 6 * fb + 6)
                        wait(dve, facc_s, NX * NT * fb + NT * (e - 1))
                        for i in range(NT):
                            w.scalar_tensor_tensor(facc[:, i, :], F2[:, i * D:i * D + D],
                                                   wts[:, i, ORDER[e]:ORDER[e] + 1], facc[:, i, :],
                                                   ALU.mult, ALU.add).then_inc(facc_s, 1)

            def side(b, slot, prep_b, prep_f, post_f):
                if post_f and slot in (POST_F_SLOT, POST_F_SLOT + 1):
                    skip_add(b, 0, slot - POST_F_SLOT)
                if prep_f is not None:
                    norms(prep_f, slot)
                    prep(prep_f, 0, slot - PREP_F_SLOT)
                if prep_b:
                    prep(b, 1, slot - PREP_B_SLOT)

            for slot in range(STEPS):
                side(-1, slot, False, 0, False)
            dve.wait_ge(const_ok, CONSTS)

            def body(b, scan_, ffn, last):
                for slot in range(STEPS):
                    step = STEPS * b + slot
                    if scan_:
                        scan(step, slot // N, slot % N)
                    if slot > 0 and scan_:
                        read_out(step - 1, (slot - 1) // N, (slot - 1) % N, b)
                    elif slot == 0 and ffn:
                        read_out(step - 1, 1, N - 1, b - 1)
                    if scan_:
                        side(b, slot, True, None if last else b + 1, True)
                    if ffn:
                        ffn_side(b - 1, slot)

            passes(dve, body)

        @block.tensor
        def _(pe):
            m = nc.tensor
            pe.wait_ge(ident_ok, 2)
            pe.wait_ge(loaded, LOADS)
            for d in range(2):
                pe.wait_ge(taps_ok, NH * TAPS * (d + 1))
                if d:
                    pe.wait_ge(wt_ev, 5)
                for half in range(NH):
                    for j in range(TAPS):
                        col = (half * TAPS + j) * P
                        m.transpose(psB[:, col:col + P], win_tap[d][:, half, j, :], ident[:, :])
                    m.transpose(psH[:, half * P:half * P + P], win_nat[d][:, NH + half, :], ident[:, :])
                    k = R + 2 * N
                    m.transpose(psH[:, (2 + half) * P:(2 + half) * P + k], wx_nat[d][:, half * P:half * P + P],
                                ident[0:k, 0:k])
                    m.transpose(psH[0:R, (4 + half) * P:(5 + half) * P], wdt_nat[d][:, half, :], ident[:, :])
                    last = m.transpose(psH[:, (6 + half) * P:(7 + half) * P], wout_nat[d][:, half * P:half * P + P],
                                       ident[:, :])
                last.then_inc(wt_tr, 1)
            pe.wait_ge(c_step, 2)
            m.transpose(F0[:, 0:NB], c_silu[:, :], ident[0:NB, 0:NB]).then_inc(c_step, 1)
            pe.wait_ge(c_step, 4)
            m.matmul(F0[0:NB, :], cT[:, :], wmod[:, 0:T], start=True, stop=True)
            m.matmul(F1[0:NB, 0:2 * D], cT[:, :], wmod[:, T:KINDS * D], start=True, stop=True).then_inc(mod_mm, 1)
            pe.wait_ge(mod_v, KINDS)
            pe.wait_ge(wt_ev, 10)
            pe.wait_ge(halved, 7)

            def tr_b(step, n):
                pe.wait_ge(bt_s, step + 1)
                wait(pe, h_s, step)
                for half in range(NH):
                    for i in range(NT):
                        last = m.transpose(psB[:, half * T + i * P:half * T + i * P + P],
                                           bt[:, n % 2, i, half * P:half * P + P], ident[:, :])
                last.then_inc(pB_full, 1)

            def tr_h(step, n):
                pe.wait_ge(h_s, step + 1)
                wait(pe, acc_s, NT * step)
                for i in range(NT):
                    for half in range(NH):
                        last = m.transpose(psH[:, i * E + half * P:i * E + half * P + P],
                                           h[:, n % 2, half, i * P:i * P + P], ident[:, :])
                last.then_inc(pH_full, 1)

            def prep(b, d, k):
                def open_piece(kind, half=0):
                    wait(pe, pP_free, PIECES * b + piece(d, kind, half))
                if k in (0, 1):
                    open_piece(U, k)
                    for j in range(TAPS):
                        lo = j if d == 0 else 2 * PAD - j
                        last = m.matmul(psP[:, :], wcT[d][:, k, j, :], xnT[:, lo:lo + T],
                                        start=(j == 0), stop=(j == TAPS - 1))
                    last.then_inc(pP_full, 1)
                if k == 2:
                    pe.wait_ge(silu_s, 8 * b + 4 * d + 2)
                    open_piece(DTR)
                    for half in range(NH):
                        last = m.matmul(psP[0:R, :], wxT[d][:, half, 0:R], u[d][:, half, :],
                                        start=(half == 0), stop=(half == NH - 1))
                    last.then_inc(pP_full, 1)
                    open_piece(BCP)
                    for i in range(NT):
                        for half in range(NH):
                            last = m.matmul(psP[:, i * 2 * N:(i + 1) * 2 * N], u[d][:, half, i * P:i * P + P],
                                            wxT[d][:, half, R:R + 2 * N], start=(half == 0), stop=(half == NH - 1))
                    last.then_inc(pP_full, 1)
                if k in (3, 4):
                    open_piece(DT, k - 3)
                    m.matmul(psP[:, :], wdtT[d][:, k - 3, :], dtr[:, :], start=True, stop=True).then_inc(pP_full, 1)
                if k in (6, 7):
                    pe.wait_ge(v_s, 2 * b + d + 1)
                    open_piece(VT, k - 6)
                    for i in range(NT):
                        last = m.transpose(psP[:, i * P:i * P + P], v[:, k - 6, i * P:i * P + P], ident[:, :])
                    last.then_inc(pP_full, 1)
                if k in (8, 9):
                    open_piece(Z, k - 8)
                    m.matmul(psP[:, :], wzT[d][:, k - 8, :], xnT[:, PAD:PAD + T], start=True, stop=True)\
                        .then_inc(pP_full, 1)

            def side(b, slot, prep_b, prep_f, post_f):
                if post_f and slot in (POST_F_SLOT, POST_F_SLOT + 1):
                    half = slot - POST_F_SLOT
                    pe.wait_ge(acc_s, NT * (STEPS * b + N))
                    wait(pe, pP_free, PIECES * b + POSTF + half)
                    for i in range(NT):
                        last = m.transpose(psP[:, i * P:i * P + P], acc[0][:, i, half * P:half * P + P], ident[:, :])
                    last.then_inc(pP_full, 1)
                if prep_f is not None:
                    if slot == LN_SLOT + 3:
                        pe.wait_ge(zA, 8 * prep_f + 8)
                        wait(pe, pP_free, PIECES * prep_f)
                        for i in range(NT):
                            last = m.transpose(psP[:, i * P:i * P + P], xn[:, i, :], ident[:, :])
                        last.then_inc(pP_full, 1)
                    prep(prep_f, 0, slot - PREP_F_SLOT)
                if prep_b:
                    prep(b, 1, slot - PREP_B_SLOT)

            def ffn_side(fb, slot):
                full = (DOWN + NE) * fb
                free = (DOWN + 1) * fb
                if slot in (1, 2):
                    half = slot - 1
                    if half == 0:
                        pe.wait_ge(acc_s, NT * (STEPS * fb + STEPS))
                        wait(pe, facc_s, NX * NT * fb)
                    else:
                        pe.wait_ge(F2_free, free + POSTB + half)
                    for i in range(NT):
                        last = m.transpose(F2[:, i * P:i * P + P], acc[1][:, i, half * P:half * P + P], ident[:, :])
                    last.then_inc(F2_full, 1)
                if slot == 3:
                    for d in range(2):
                        pe.wait_ge(yg_s[d], NH * fb + NH)
                    pe.wait_ge(F2_free, free + PROJ)
                    for i in range(NT):
                        for k in range(2 * NH):
                            last = m.matmul(F2[:, i * D:i * D + D], yg[k // NH][:, k % NH, i * P:i * P + P],
                                            woutT[k // NH][:, k % NH, :], start=(k == 0), stop=(k == 2 * NH - 1))
                    last.then_inc(F2_full, 1)
                if slot == 5:
                    pe.wait_ge(h2_s, 2 * fb + 2)
                    pe.wait_ge(F2_free, free + H2T)
                    for i in range(NT):
                        last = m.transpose(F2[:, i * P:i * P + P], h2[:, i, :], ident[:, :])
                    last.then_inc(F2_full, 1)
                if slot == 6:
                    pe.wait_ge(F2_free, free + GATE)
                    for i in range(NT):
                        last = m.matmul(F2[:, i * NX:(i + 1) * NX], h2T[:, i * P:i * P + P], gate_w[:, :],
                                        start=True, stop=True)
                    last.then_inc(F2_full, 1)
                experts(fb, slot, "up")

            def experts(fb, slot, part_):
                free = (DOWN + 1) * fb
                for kind, e, half in EXPERT_AT.get(slot, ()):
                    x_ = ORDER[e]
                    if kind != part_:
                        continue
                    if kind == "up":
                        k = 2 * NE * fb + 2 * e + half
                        wait(pe, pf_s, k)
                        m.matmul(F0[:, :], w1[:, x_, half * P:half * P + P], h2T[:, :], start=True, stop=True)\
                            .then_inc(F0_full, 1)
                        wait(pe, act_s, k)
                        m.matmul(F1[:, :], w2[:, x_, half * P:half * P + P], h2T[:, :], start=True, stop=True)\
                            .then_inc(F1_full, 1)
                    else:
                        pe.wait_ge(act_s, 2 * NE * fb + 2 * e + 2)
                        if e <= 1:
                            pe.wait_ge(F2_free, free + DOWN + e)
                        else:
                            pe.wait_ge(facc_s, NX * NT * fb + NT * (e - 1))
                        for i in range(NT):
                            for half2 in range(2):
                                last = m.matmul(F2[:, i * D:i * D + D], act[:, half2, i * P:i * P + P],
                                                w3[:, x_, half2, :], start=(half2 == 0), stop=(half2 == 1))
                        last.then_inc(F2_full, 1)

            for slot in range(STEPS):
                side(-1, slot, False, 0, False)

            def body(b, scan_, ffn, last):
                for slot in range(STEPS):
                    step = STEPS * b + slot
                    if scan_:
                        tr_b(step, slot % N)
                    if ffn:
                        ffn_side(b - 1, slot)
                    if (slot > 0 and scan_) or (slot == 0 and ffn):
                        tr_h(step - 1, (slot - 1) % N)
                    if ffn:
                        experts(b - 1, slot, "down")
                    if scan_:
                        side(b, slot, True, None if last else b + 1, True)

            passes(pe, body)


_NAMES = {
    "L0_attn_x": "x", "L0_attn_norm_g": "norm_g", "L0_attn_norm_b": "norm_b", "L0_ffn_gate_w": "gate_w",
    "L0_ffn_ew1": "ew1", "L0_ffn_ew2": "ew2", "L0_ffn_ew3": "ew3", "L0_ffn_sw1": "sw1", "L0_ffn_sw2": "sw2",
    "L0_ffn_sw3": "sw3", "L0_c": "c", "L0_wmod": "wmod",
}
_DIR = ["Win", "convw", "convb", "Wx", "Wdt", "bdt", "Alog", "D", "Wout"]


def kernel(**inputs):
    import numpy as _np
    import concourse.bacc as _bacc
    from concourse import mybir as _mybir
    from concourse.bass_utils import run_bass_kernel_spmd as _run

    nc = _bacc.Bacc("TRN2", target_bir_lowering=False, num_devices=1)
    arrays = {}

    def given(name):
        arr = _np.ascontiguousarray(inputs[name])
        arrays[f"in_{name}"] = arr
        return nc.dram_tensor(f"in_{name}", arr.shape, _mybir.dt.from_np(arr.dtype), kind="ExternalInput").ap()

    t = {short: given(name) for name, short in _NAMES.items()}
    for d in "fb":
        t[d] = {w: given(f"L0_attn_{d}_{w}") for w in _DIR}
    out = nc.dram_tensor("out_x", (NB, T, D), _mybir.dt.float32, kind="ExternalOutput").ap()
    adaln_mamba_moe(nc, t, out)
    r = _run(nc, [arrays], core_ids=[0])
    return r.results[0]["out_x"]
```

```python
import concourse.bass as bass
from concourse import mybir
from contextlib import ExitStack

NB, T, D = 16, 512, 128
P = 128
NT = T // P
E = 2 * D
NH = E // P
N = 16
R = 8
TAPS = 4
NX = 8
NE = NX + 1
HID = 2 * D
EPS = 1e-5
STEPS = 2 * N
PAD = TAPS - 1
KINDS = 6

XN = 0
U, Z, XD, DT, CP = 0, 2, 4, 5, 7
PREP = 8
POSTF = 1 + 2 * PREP
PIECES = POSTF + NH
POSTB, PROJ, H2T, GATE, DOWN = 0, 2, 3, 4, 5

PREP_SLOT = (21, 1)
U_AT, Z_AT, XD_AT, DT_AT, CP_AT, V_AT = 0, 2, 4, 5, 7, 9
LN_SLOT, XN_SLOT, RES_SLOT = 13, 20, 20
POST_F_SLOT = 17
POSTB_SLOT, PROJ_SLOT, FX_SLOT, LN3_SLOT, H2T_SLOT, GATE_SLOT = 1, 4, 6, 7, 10, 11
UP_SLOT, DOWN_SLOT = 11, 14


def piece(d, kind, half=0):
    return 1 + PREP * d + kind + half


def up_at(slot):
    k = slot - UP_SLOT
    return k if 0 <= k < 2 * NE else None


def down_at(slot):
    e, odd = divmod(slot - DOWN_SLOT, 2)
    return e if 0 <= e < NE and not odd else None


ORDER = [NX] + list(range(NX))


def adaln_mamba_moe(nc, t, out):
    f32, u32 = mybir.dt.float32, mybir.dt.uint32
    ALU, ACT = mybir.AluOpType, mybir.ActivationFunctionType
    ctx = ExitStack()
    with ctx:
        def sb(name, shape, dt=f32):
            return ctx.enter_context(nc.sbuf_tensor(name, shape, dt))

        def ps(name, shape):
            return ctx.enter_context(nc.psum_tensor(name, shape, f32))

        def sem(name):
            return ctx.enter_context(nc.semaphore(name))

        ident = sb("ident", [P, P])
        iota8 = sb("iota8", [P, NX])
        wdt_nat = [sb(f"wdt_nat{d}", [P, NH, R]) for d in range(2)]
        convw = [sb(f"convw{d}", [P, NH, TAPS]) for d in range(2)]
        convb = [sb(f"convb{d}", [P, NH]) for d in range(2)]
        bdt = [sb(f"bdt{d}", [P, NH]) for d in range(2)]
        skip = [sb(f"skip{d}", [P, NH]) for d in range(2)]
        alog = [sb(f"alog{d}", [P, NH, N]) for d in range(2)]
        aneg = [sb(f"aneg{d}", [P, NH, N]) for d in range(2)]
        wcT = [sb(f"wcT{d}", [D, NH, TAPS, P]) for d in range(2)]
        wzT = [sb(f"wzT{d}", [D, NH, P]) for d in range(2)]
        wxT = [sb(f"wxT{d}", [P, NH, R + 2 * N]) for d in range(2)]
        wdtT = [sb(f"wdtT{d}", [R, NH, P]) for d in range(2)]
        woutT = [sb(f"woutT{d}", [P, NH, D]) for d in range(2)]
        norm = sb("norm", [P, 2])
        gate_w = sb("gate_w", [D, NX])
        w1 = sb("w1", [D, NE, HID])
        w2 = sb("w2", [D, NE, HID])
        w3 = sb("w3", [P, NE, 2, D])
        c_nat = sb("c_nat", [NB, D])
        c_th = sb("c_th", [NB, D])
        c_silu = sb("c_silu", [NB, D])
        cT = sb("cT", [D, NB])
        gsgn = sb("gsgn", [NB, 2, D])
        gabs = sb("gabs", [NB, 2, D])
        modA = sb("modA", [P, 3, D])
        modF = sb("modF", [P, 4, D])
        x = sb("x", [P, NT, D])
        st = sb("st", [P, NT, 6])
        stat = sb("stat", [P, NT, 6])
        mhalf = sb("mhalf", [P, NT])
        rstd = sb("rstd", [P, NT])
        z1 = sb("z1", [P, NT, D])
        xn = sb("xn", [P, NT, D])
        xnT = sb("xnT", [D, T + 2 * PAD])
        rN = sb("rN", [P, NT, D])
        rC = sb("rC", [P, NT, D])
        xh = sb("xh", [P, 4, T])
        th = sb("th", [P, 4, T])
        u = [sb(f"u{d}", [P, NH, T]) for d in range(2)]
        zs = [sb(f"zs{d}", [P, NH, T]) for d in range(2)]
        xd = sb("xd", [R + N, T])
        cc = [sb(f"cc{d}", [P, NT, N]) for d in range(2)]
        xb = sb("xb", [P, NH, T])
        ab = sb("ab", [P, NH, T])
        dt_ = [sb(f"dt{d}", [P, NH, T]) for d in range(2)]
        v = [sb(f"v{d}", [P, NH, T]) for d in range(2)]
        bb = sb("bb", [P, 2, 2, T])
        bt = sb("bt", [P, 2, NH, T])
        zero = sb("zero", [P, NH, 1])
        h = sb("h", [P, 2, NH, T])
        acc = [sb(f"acc{d}", [P, NT, E]) for d in range(2)]
        def part(buf, rows, lo, shape):
            flat = buf.rearrange("p a b c -> p (a b c)") if len(buf.shape) == 4 else buf.rearrange("p a b -> p (a b)")
            size = 1
            for k in shape:
                size *= k
            flat = flat[0:rows, lo:lo + size]
            if len(shape) == 1:
                return flat
            if len(shape) == 2:
                return flat.rearrange("p (a b) -> p a b", b=shape[1])
            return flat.rearrange("p (a b c) -> p a b c", b=shape[1], c=shape[2])

        win_tap = [part(bt[:, :, :, :], P, d * NH * TAPS * D, [NH, TAPS, D]) for d in range(2)]
        win_nat = [part(h[:, :, :, :], P, d * 4 * D, [4, D]) for d in range(2)]
        wx_nat = [part(h[:, :, :, :], R + 2 * N, 8 * D + d * E, [E]) for d in range(2)]
        wout_nat = [part(h[:, :, :, :], D, 12 * D + d * E, [E]) for d in range(2)]
        wmod = part(acc[0][:, :, :], D, 0, [KINDS * D])
        mod = part(acc[1][:, :, :], NB, 0, [KINDS, D])
        yt = [sb(f"yt{d}", [P, T]) for d in range(2)]
        yg = [sb(f"yg{d}", [P, NH, T]) for d in range(2)]
        fx = sb("fx", [P, NT, D])
        x2 = sb("x2", [P, NT, D])
        stF = sb("stF", [P, NT, 6])
        statF = sb("statF", [P, NT, 6])
        rstdF = sb("rstdF", [P, NT])
        zF = sb("zF", [P, NT, D])
        h2T = sb("h2T", [D, T])
        gl = sb("gl", [P, NT, NX])
        gl2 = sb("gl2", [P, NT, NX])
        top = sb("top", [P, NT, NX])
        topi = sb("topi", [P, NT, NX], u32)
        topf = sb("topf", [P, NT, 2])
        gd = sb("gd", [P, NT])
        ge = sb("ge", [P, NT])
        gs = sb("gs", [P, NT])
        gw = sb("gw", [P, 2, NT])
        hot = sb("hot", [P, 2, NT, NX])
        hotw = sb("hotw", [P, 2, NT, NX])
        wts = sb("wts", [P, NT, NX])
        tf = sb("tf", [P, 2, T])
        hf = sb("hf", [P, 2, T])
        gf = sb("gf", [P, 3, T])
        pf = sb("pf", [P, 2, T])
        act = sb("act", [P, 2, 2, T])
        facc = sb("facc", [P, NT, D])
        osb = sb("osb", [P, NT, D])

        psA = ps("psA", [P, NH * T])
        psH = ps("psH", [P, NT * E])
        psP = ps("psP", [P, T])
        F0 = ps("F0", [P, T])
        F1 = ps("F1", [P, T])
        F2 = ps("F2", [P, T])

        b_dram = nc.dram_tensor("b_rows", (2, N, T), f32, kind="Internal").ap()
        mod_dram = nc.dram_tensor("mod_table", (NB, KINDS * D), f32, kind="Internal").ap()

        loaded = sem("loaded")
        const_ok = sem("const_ok")
        ident_ok = sem("ident_ok")
        taps_ok = sem("taps_ok")
        wt_tr = sem("wt_tr")
        wt_ev = sem("wt_ev")
        halved = sem("halved")
        c_step = sem("c_step")
        mod_mm = sem("mod_mm")
        mod_v = sem("mod_v")
        mod_out = sem("mod_out")
        x_in = sem("x_in")
        modA_in = sem("modA_in")
        lnA = sem("lnA")
        rstdA = sem("rstdA")
        zA = sem("zA")
        h1_s = sem("h1_s")
        rN_s = sem("rN_s")
        rC_s = sem("rC_s")
        pP_full = sem("pP_full")
        pP_free = sem("pP_free")
        th_s = sem("th_s")
        silu_s = sem("silu_s")
        sp_s = sem("sp_s")
        dt_s = sem("dt_s")
        v_s = sem("v_s")
        brow_out = sem("brow_out")
        bb_in = [sem(f"bb_in{k}") for k in range(2)]
        bt_s = sem("bt_s")
        a_s = sem("a_s")
        h_s = sem("h_s")
        pH_full = sem("pH_full")
        acc_s = sem("acc_s")
        yg_s = [sem("yg_f_s"), sem("yg_b_s")]
        modF_in = sem("modF_in")
        F2_full = sem("F2_full")
        F2_free = sem("F2_free")
        x2_s = sem("x2_s")
        lnF = sem("lnF")
        rstdF_s = sem("rstdF_s")
        zF_s = sem("zF_s")
        h2_s = sem("h2_s")
        gate_s = sem("gate_s")
        ge_s = sem("ge_s")
        F0_full = sem("F0_full")
        F1_full = sem("F1_full")
        F0_free = sem("F0_free")
        F1_free = sem("F1_free")
        pf_s = sem("pf_s")
        act_s = sem("act_s")
        facc_s = sem("facc_s")
        gw_s = sem("gw_s")
        o_s = sem("o_s")
        out_d = sem("out_d")
        GATES = 13
        GATE_D = 6
        LOADS = 16 * 29
        MOD_STEPS = 12
        CONSTS = 5

        block = ctx.enter_context(nc.Block())

        def wait(eng, s, value):
            if not (isinstance(value, int) and value <= 0):
                eng.wait_ge(s, value)

        def passes(eng, body):
            body(0, True, False, False)
            body(1, True, True, False)
            with eng.Fori(2, NB - 1) as b:
                body(b, True, True, False)
            body(NB - 1, True, True, True)
            body(NB, False, True, True)

        @block.sync
        def _(sp):
            small = nc.allow_non_contiguous_dma(reason="small weight columns")
            with small:
                for d in range(2):
                    w = t["fb"[d]]
                    for dst, src in (
                        (win_nat[d][:, :, :], w["Win"].rearrange("(k p) d -> p k d", p=P)),
                        (wx_nat[d][:, :], w["Wx"]),
                        (wdt_nat[d][:, :, :], w["Wdt"].rearrange("(k p) r -> p k r", p=P)),
                        (wout_nat[d][:, :], w["Wout"]),
                        (convw[d][:, :, :], w["convw"].rearrange("(k p) a j -> p k (a j)", p=P)),
                        (convb[d][:, :], w["convb"].rearrange("(k p) -> p k", p=P)),
                        (bdt[d][:, :], w["bdt"].rearrange("(k p) -> p k", p=P)),
                        (skip[d][:, :], w["D"].rearrange("(k p) -> p k", p=P)),
                        (alog[d][:, :, :], w["Alog"].rearrange("(k p) n -> p k n", p=P)),
                        (norm[:, d:d + 1], t["norm_g" if d == 0 else "norm_b"].rearrange("(p a) -> p a", a=1)),
                    ):
                        sp.dma_start(dst, src).then_inc(loaded, 16)
                for dst, src in (
                    (c_nat[:, :], t["c"]),
                    (wmod[:, :], t["wmod"]),
                    (gate_w[:, :], t["gate_w"]),
                    (w1[:, 0:NX, :], t["ew1"].rearrange("e d h -> d e h")),
                    (w2[:, 0:NX, :], t["ew2"].rearrange("e d h -> d e h")),
                    (w3[:, 0:NX, :, :], t["ew3"].rearrange("e (k p) d -> p e k d", p=P)),
                    (w1[:, NX, :], t["sw1"]),
                    (w2[:, NX, :], t["sw2"]),
                    (w3[:, NX, :, :], t["sw3"].rearrange("(k p) d -> p k d", p=P)),
                ):
                    sp.dma_start(dst, src).then_inc(loaded, 16)
            sp.wait_ge(mod_v, MOD_STEPS)
            sp.dma_start(mod_dram, mod[:, :, :].rearrange("b k d -> b (k d)")).then_inc(mod_out, 16)
            sp.wait_ge(mod_out, 16)

            def load(b):
                wait(sp, rN_s, 2 * b)
                sp.dma_start(x[:, :, :], t["x"][bass.ds(b, 1)].rearrange("a (k p) d -> p (a k) d", p=P))\
                    .then_inc(x_in, 16)
                row = mod_dram[bass.ds(b, 1), 0:3 * D].broadcast_to([P, 3 * D])
                sp.dma_start(modA[:, :, :].rearrange("p k d -> p (k d)"), row).then_inc(modA_in, 16)

            def rows_out(b, d):
                sp.wait_ge(pP_free, PIECES * b + piece(d, XD) + 1)
                sp.dma_start(b_dram[d], xd[R:R + N, :]).then_inc(brow_out, 16)

            def rows_in(b, d, pair):
                used = 2 * (N * b + N * d // 2 + pair - 1)
                if pair == 0:
                    sp.wait_ge(brow_out, 16 * (2 * b + d + 1))
                wait(sp, bt_s, used)
                src = b_dram[d, 2 * pair:2 * pair + 2, :].rearrange("n t -> (n t)").unsqueeze(0)
                sp.dma_start(bb[:, pair % 2, :, :].rearrange("p n t -> p (n t)"), src.broadcast_to([P, 2 * T]))\
                    .then_inc(bb_in[pair % 2], 16)

            load(0)
            rows_out(0, 0)
            rows_in(0, 0, 0)
            rows_in(0, 0, 1)

            def body(b, scan, ffn, last):
                for slot in range(STEPS):
                    if scan and slot == PREP_SLOT[1] + XD_AT + 1:
                        rows_out(b, 1)
                    if scan and not last and slot == PREP_SLOT[0] + XD_AT + 1:
                        rows_out(b + 1, 0)
                    if slot % 2 == 0:
                        step = slot + 4
                        if scan and step < STEPS:
                            rows_in(b, step // N, step % N // 2)
                        elif scan and not last:
                            rows_in(b + 1, 0, (step - STEPS) // 2)
                    if slot == 0:
                        early(b, scan, ffn, last)
                    if slot == 0 and not (isinstance(b, int) and b < 2):
                        store(b - 2)

            def early(b, scan, ffn, last):
                if ffn:
                    fb = b - 1
                    wait(sp, o_s, 2 * fb)
                    row = mod_dram[bass.ds(fb, 1), 2 * D:6 * D].broadcast_to([P, 4 * D])
                    sp.dma_start(modF[:, :, :].rearrange("p k d -> p (k d)"), row).then_inc(modF_in, 16)
                if scan and not last:
                    load(b + 1)

            def store(fb):
                sp.wait_ge(o_s, 2 * fb + 2)
                sp.dma_start(out[bass.ds(fb, 1)].rearrange("a (k p) d -> p (a k) d", p=P), osb[:, :, :])\
                    .then_inc(out_d, 16)

            passes(sp, body)
            store(NB - 1)
            sp.wait_ge(out_d, 16 * NB)

        @block.gpsimd
        def _(pool):
            g = nc.gpsimd
            g.memset(ident[:, :], 0.0).then_inc(ident_ok, 1)
            pool.wait_ge(ident_ok, 1)
            g.affine_select(out=ident[:, :], in_=ident[:, :], compare_op=ALU.not_equal, fill=1.0, base=0,
                            pattern=[[-1, P]], channel_multiplier=1).then_inc(ident_ok, 1)
            g.iota(iota8[:, :], pattern=[[1, NX]], base=0, channel_multiplier=0,
                   allow_small_or_imprecise_dtypes=True).then_inc(const_ok, 1)
            g.memset(mhalf[:, :], -0.5).then_inc(const_ok, 1)

            def over_tiles(row):
                return row.unsqueeze(1).broadcast_to([P, NT, D])

            def bmul(step, d, n):
                wait(pool, h_s, step - 1)
                if n == 0:
                    pool.wait_ge(v_s, bmul.unit)
                if n % 2 == 0:
                    pool.wait_ge(bb_in[n // 2 % 2], 64 * bmul.unit + 16 * (n // 4) - 48)
                g.tensor_tensor(bt[:, n % 2, :, :], v[d][:, :, :],
                                bb[:, n // 2 % 2, n % 2, :].unsqueeze(1).broadcast_to([P, NH, T]),
                                ALU.mult).then_inc(bt_s, 1)

            def rsqrt(dst, src):
                return g.tensor_tensor(dst, src, mhalf[:, :], ALU.pow)

            def norms(b, slot):
                if slot == LN_SLOT + 1:
                    if isinstance(b, int) and b == 0:
                        pool.wait_ge(const_ok, CONSTS)
                    pool.wait_ge(lnA, 20 * b + 10)
                    rsqrt(rstd[:, :], stat[:, :, 3]).then_inc(rstdA, 1)
                if slot == LN_SLOT + 3:
                    pool.wait_ge(zA, 8 * b + 4)
                    pool.wait_ge(modA_in, 16 * b + 16)
                    wait(pool, pP_full, PIECES * (b - 1) + XN + 1)
                    g.tensor_tensor(xn[:, :, :], z1[:, :, :], over_tiles(modA[:, 1, :]), ALU.mult).then_inc(h1_s, 1)
                    pool.wait_ge(h1_s, 2 * b + 1)
                    g.tensor_tensor(z1[:, :, :], xn[:, :, :], over_tiles(modA[:, 0, :]), ALU.add).then_inc(h1_s, 1)
                if slot == LN_SLOT + 5:
                    pool.wait_ge(lnA, 20 * b + 20)
                    rsqrt(rstd[:, :], stat[:, :, 3]).then_inc(rstdA, 1)
                if slot == RES_SLOT:
                    wait(pool, rC_s, b)
                    g.tensor_tensor(rN[:, :, :], z1[:, :, :], over_tiles(modA[:, 2, :]), ALU.mult).then_inc(rN_s, 1)
                    pool.wait_ge(rN_s, 2 * b + 1)
                    pool.wait_ge(x_in, 16 * b + 16)
                    g.tensor_tensor(rN[:, :, :], rN[:, :, :], x[:, :, :], ALU.add).then_inc(rN_s, 1)

            def make_v(b, d):
                pool.wait_ge(dt_s, 2 * b + d + 1)
                wait(pool, bt_s, STEPS * (b - 1) + N * (d + 1))
                g.tensor_tensor(v[d][:, :, :], u[d][:, :, :], dt_[d][:, :, :], ALU.mult).then_inc(v_s, 1)

            def output(fb):
                pool.wait_ge(facc_s, NX * NT * fb + NX * NT)
                g.tensor_tensor(fx[:, :, :], facc[:, :, :], over_tiles(modF[:, 3, :]), ALU.mult).then_inc(o_s, 1)
                pool.wait_ge(o_s, 2 * fb + 1)
                wait(pool, out_d, 16 * fb)
                g.tensor_tensor(osb[:, :, :], fx[:, :, :], x2[:, :, :], ALU.add).then_inc(o_s, 1)

            def gate_y(b, d, half):
                if d == 0:
                    pool.wait_ge(pP_free, PIECES * b + POSTF + half + 1)
                    wait(pool, F2_full, (DOWN + NE) * (b - 1) + PROJ + 1)
                else:
                    pool.wait_ge(F2_free, (DOWN + 1) * b + POSTB + half + 1)
                g.tensor_tensor(yg[d][:, half, :], yt[d][:, :], zs[d][:, half, :], ALU.mult).then_inc(yg_s[d], 1)

            def ffn_side(fb, slot):
                if slot - POSTB_SLOT in (1, 2):
                    gate_y(fb, 1, slot - POSTB_SLOT - 1)
                if slot == FX_SLOT:
                    pool.wait_ge(F2_free, (DOWN + 1) * fb + PROJ + 1)
                    pool.wait_ge(rC_s, fb + 1)
                    wait(pool, o_s, 2 * fb)
                    g.tensor_tensor(x2[:, :, :], fx[:, :, :], rC[:, :, :], ALU.add).then_inc(x2_s, 1)
                if slot == LN3_SLOT:
                    pool.wait_ge(lnF, 10 * fb + 10)
                    rsqrt(rstdF[:, :], statF[:, :, 3]).then_inc(rstdF_s, 1)
                if slot == LN3_SLOT + 1:
                    pool.wait_ge(zF_s, NT * fb + NT)
                    g.tensor_tensor(fx[:, :, :], zF[:, :, :], over_tiles(modF[:, 2, :]), ALU.mult).then_inc(h2_s, 1)
                    pool.wait_ge(h2_s, 2 * fb + 1)
                    g.tensor_tensor(zF[:, :, :], fx[:, :, :], over_tiles(modF[:, 1, :]), ALU.add).then_inc(h2_s, 1)
                k = up_at(slot - 1)
                if k is not None:
                    at = 2 * NE * fb + k
                    pool.wait_ge(pf_s, at + 1)
                    pool.wait_ge(F1_free, at + 1)
                    wait(pool, F2_full, (DOWN + NE) * fb + DOWN + k // 2 - 1 if k >= 4 else (DOWN + NE) * fb)
                    g.tensor_tensor(act[:, k // 2 % 2, k % 2, :], pf[:, k % 2, :], gf[:, k % 3, :], ALU.mult)\
                        .then_inc(act_s, 1)

            def side(b, slot, prep_b, prep_f, post_f):
                if post_f and slot - POST_F_SLOT in (2, 3):
                    gate_y(b, 0, slot - POST_F_SLOT - 2)
                if prep_f is not None:
                    norms(prep_f, slot)
                    if slot == PREP_SLOT[0] + V_AT:
                        make_v(prep_f, 0)
                if prep_b and slot == PREP_SLOT[1] + V_AT:
                    make_v(b, 1)

            for slot in range(STEPS):
                side(-1, slot, False, 0, False)
            bmul.unit = 1
            bmul(0, 0, 0)

            def body(b, scan, ffn, last):
                for slot in range(STEPS):
                    if scan:
                        nxt = slot + 1
                        if nxt < STEPS:
                            bmul.unit = 2 * b + 1 + nxt // N
                            bmul(STEPS * b + nxt, nxt // N, nxt % N)
                        elif not last:
                            bmul.unit = 2 * b + 3
                            bmul(STEPS * b + nxt, 0, 0)
                    if slot == 0 and not (isinstance(b, int) and b < 2):
                        output(b - 2)
                    if scan:
                        side(b, slot, True, None if last else b + 1, True)
                    if ffn:
                        ffn_side(b - 1, slot)

            passes(pool, body)
            output(NB - 1)

        @block.scalar
        def _(act_e):
            s = nc.scalar
            act_e.wait_ge(loaded, LOADS)
            s.activation(c_th[:, :], c_nat[:, :], ACT.Tanh, scale=0.5).then_inc(c_step, 1)
            for d in range(2):
                s.activation(aneg[d][:, :, :], alog[d][:, :, :], ACT.Exp).then_inc(halved, 1)
            act_e.wait_ge(halved, 2)
            for d in range(2):
                s.activation(aneg[d][:, :, :], aneg[d][:, :, :], ACT.Copy, scale=-1.0).then_inc(halved, 1)
                s.activation(convb[d][:, :], convb[d][:, :], ACT.Copy, scale=0.5).then_inc(halved, 1)
            s.activation(w3[:, :, :, :], w3[:, :, :, :], ACT.Copy, scale=0.5).then_inc(halved, 1)
            for d in range(2):
                act_e.wait_ge(wt_tr, d + 1)
                s.activation(wcT[d][:, :, :, :], psA[:, 0:NH * TAPS * P], ACT.Copy).then_inc(wt_ev, 1)
                s.activation(wzT[d][:, :, :], psH[:, 0:NH * P], ACT.Copy).then_inc(wt_ev, 1)
                s.activation(wxT[d][:, :, :], psH[:, 2 * P:4 * P].rearrange("p (k c) -> p k c", c=P)[:, :, 0:R + 2 * N],
                             ACT.Copy).then_inc(wt_ev, 1)
                s.activation(wdtT[d][:, :, :], psH[0:R, 4 * P:6 * P], ACT.Copy).then_inc(wt_ev, 1)
                s.activation(woutT[d][:, :, :], psH[:, 6 * P:8 * P], ACT.Copy).then_inc(wt_ev, 1)
            act_e.wait_ge(c_step, 3)
            s.activation(cT[:, :], F0[:, 0:NB], ACT.Copy).then_inc(c_step, 1)
            act_e.wait_ge(halved, 7)

            def exps(step, b, d, n):
                wait(act_e, h_s, step)
                lo, hi, first = (1, T, 0) if d == 0 else (0, T - 1, T - 1)
                decay = psA[:, :].rearrange("p (k t) -> p k t", t=T)
                if n == 0:
                    act_e.wait_ge(dt_s, 2 * b + d + 1)
                    s.activation(decay[:, :, first:first + 1], zero[:, :, :], ACT.Copy).then_inc(a_s, 1)
                for half in range(NH):
                    s.activation(decay[:, half, lo:hi], dt_[d][:, half, lo:hi], ACT.Exp,
                                 scale=aneg[d][:, half, n:n + 1]).then_inc(a_s, 1)

            def take(b, pos):
                act_e.wait_ge(pP_full, PIECES * b + pos + 1)

            def silu(b, d, kind, half):
                k = 8 * b + 4 * d + kind + half
                at = kind + half
                take(b, piece(d, kind, half))
                wait(act_e, silu_s, k - 3)
                if kind == U:
                    s.activation(xh[:, at, :], psP[:, :], ACT.Identity, scale=0.5,
                                 bias=convb[d][:, half:half + 1]).then_inc(pP_free, 1)
                else:
                    s.activation(xh[:, at, :], psP[:, :], ACT.Copy, scale=0.5).then_inc(pP_free, 1)
                act_e.wait_ge(pP_free, PIECES * b + piece(d, kind, half) + 1)
                s.activation(th[:, at, :], xh[:, at, :], ACT.Tanh).then_inc(th_s, 1)

            def prep(b, d, k):
                if k - U_AT in (0, 1):
                    silu(b, d, U, k - U_AT)
                if k == XD_AT:
                    take(b, piece(d, XD))
                    wait(act_e, brow_out, 16 * (2 * b + d))
                    s.activation(xd[:, :], psP[0:R + N, :], ACT.Copy).then_inc(pP_free, 1)
                if k == CP_AT:
                    take(b, piece(d, CP))
                    s.activation(cc[d][:, :, :], psP[:, 0:NT * N], ACT.Copy).then_inc(pP_free, 1)
                if k - DT_AT in (0, 1):
                    half = k - DT_AT
                    q = 5 * (2 * b + d)
                    take(b, piece(d, DT, half))
                    wait(act_e, dt_s, 2 * b + d)
                    s.activation(xb[:, half, :], psP[:, :], ACT.Identity,
                                 bias=bdt[d][:, half:half + 1]).then_inc(pP_free, 1)
                    act_e.wait_ge(pP_free, PIECES * b + piece(d, DT, half) + 1)
                    s.activation(ab[:, half, :], xb[:, half, :], ACT.Abs).then_inc(sp_s, 1)
                    act_e.wait_ge(sp_s, q + 2 * half + 1)
                    s.activation(ab[:, half, :], ab[:, half, :], ACT.Exp, scale=-1.0).then_inc(sp_s, 1)
                    if half == 1:
                        act_e.wait_ge(sp_s, q + 4)
                        s.activation(ab[:, :, :], ab[:, :, :], ACT.Ln, bias=1.0).then_inc(sp_s, 1)
                if k - Z_AT in (0, 1):
                    silu(b, d, Z, k - Z_AT)

            def side(b, slot, prep_b, prep_f):
                if prep_f is not None:
                    if slot == XN_SLOT:
                        take(prep_f, XN)
                        s.activation(xnT[:, PAD:PAD + T], psP[:, :], ACT.Identity, scale=norm[:, 0:1],
                                     bias=norm[:, 1:2]).then_inc(pP_free, 1)
                    prep(prep_f, 0, slot - PREP_SLOT[0])
                if prep_b:
                    prep(b, 1, slot - PREP_SLOT[1])

            def ffn_side(fb, slot):
                if slot == H2T_SLOT:
                    act_e.wait_ge(F2_full, (DOWN + NE) * fb + H2T + 1)
                    s.activation(h2T[:, :], F2[:, :], ACT.Copy).then_inc(F2_free, 1)
                if slot == GATE_SLOT + 2:
                    act_e.wait_ge(gate_s, GATES * fb + GATE_D)
                    s.activation(ge[:, :], gd[:, :], ACT.Exp).then_inc(ge_s, 1)
                k = up_at(slot)
                if k is not None:
                    at = 2 * NE * fb + k
                    act_e.wait_ge(F0_full, at + 1)
                    wait(act_e, pf_s, at - 1)
                    s.activation(tf[:, k % 2, :], F0[:, :], ACT.Tanh, scale=0.5).then_inc(F0_free, 1)
                    s.activation(hf[:, k % 2, :], F0[:, :], ACT.Copy).then_inc(F0_free, 1)
                    act_e.wait_ge(F1_full, at + 1)
                    wait(act_e, act_s, at - 2)
                    s.activation(gf[:, k % 3, :], F1[:, :], ACT.Copy).then_inc(F1_free, 1)
                if down_at(slot) == 0:
                    act_e.wait_ge(F2_full, (DOWN + NE) * fb + DOWN + 1)
                    wait(act_e, o_s, 2 * fb)
                    s.activation(facc[:, :, :], F2[:, :], ACT.Copy).then_inc(F2_free, 1)

            for slot in range(STEPS):
                side(-1, slot, False, 0)
            act_e.wait_ge(const_ok, CONSTS)
            exps(0, 0, 0, 0)

            def body(b, scan, ffn, last):
                for slot in range(STEPS):
                    nxt = slot + 1
                    if scan and nxt < STEPS:
                        exps(STEPS * b + nxt, b, nxt // N, nxt % N)
                    elif scan and not last:
                        exps(STEPS * b + nxt, b + 1, 0, 0)
                    if scan:
                        if slot == FX_SLOT + 2:
                            wait(act_e, x2_s, b)
                            act_e.wait_ge(rN_s, 2 * b + 2)
                            s.activation(rC[:, :, :], rN[:, :, :], ACT.Copy).then_inc(rC_s, 1)
                    if ffn:
                        ffn_side(b - 1, slot)
                    if scan:
                        side(b, slot, True, None if last else b + 1)

            passes(act_e, body)

        @block.vector
        def _(dve):
            w = nc.vector
            w.memset(xnT[:, 0:PAD], 0.0).then_inc(const_ok, 1)
            w.memset(xnT[:, PAD + T:], 0.0).then_inc(const_ok, 1)
            w.memset(zero[:, :, :], 0.0).then_inc(const_ok, 1)
            dve.wait_ge(loaded, LOADS)
            for d in range(2):
                for half in range(NH):
                    for j in range(TAPS):
                        w.tensor_scalar(win_tap[d][:, half, j, :], win_nat[d][:, half, :],
                                        convw[d][:, half, j:j + 1], None, ALU.mult).then_inc(taps_ok, 1)
            dve.wait_ge(c_step, 1)
            w.scalar_tensor_tensor(c_silu[:, :], c_th[:, :], 1.0, c_nat[:, :], ALU.add, ALU.mult).then_inc(c_step, 1)
            dve.wait_ge(mod_mm, 1)
            for k in range(KINDS):
                src = (F0, F1)[k // 4][0:NB, (k % 4) * D:(k % 4) * D + D]
                w.tensor_scalar(mod[:, k, :], src, 0.5, 1.0 if k % 3 == 1 else 0.0, ALU.mult, ALU.add)\
                    .then_inc(mod_v, 1)
            dve.wait_ge(mod_v, KINDS)
            gates = mod[:, 2:6:3, :]
            w.tensor_scalar(gsgn[:, :, :], gates, 0.0, 2.0, ALU.is_ge, ALU.mult).then_inc(mod_v, 1)
            w.scalar_tensor_tensor(gabs[:, :, :], gates, -1.0, gates, ALU.mult, ALU.max).then_inc(mod_v, 1)
            dve.wait_ge(mod_v, KINDS + 2)
            w.tensor_scalar(gabs[:, :, :], gabs[:, :, :], 0.25, None, ALU.max).then_inc(mod_v, 1)
            w.tensor_scalar(gsgn[:, :, :], gsgn[:, :, :], -1.0, None, ALU.add).then_inc(mod_v, 1)
            dve.wait_ge(mod_v, KINDS + 4)
            for k in range(2):
                w.tensor_tensor(mod[:, 2 + 3 * k, :], gsgn[:, k, :], gabs[:, k, :], ALU.mult).then_inc(mod_v, 1)
            dve.wait_ge(mod_v, MOD_STEPS)

            def scan(step, d, n, unit):
                dve.wait_ge(a_s, NH * (step + 1) + unit)
                dve.wait_ge(bt_s, step + 1)
                wait(dve, pH_full, 2 * step - 2)
                order = slice(None) if d == 0 else slice(None, None, -1)
                w.tensor_tensor_scan(h[:, n % 2, :, :].rearrange("p k t -> p (k t)")[:, order], psA[:, order],
                                     bt[:, n % 2, :, :].rearrange("p k t -> p (k t)")[:, order],
                                     0.0, ALU.mult, ALU.add).then_inc(h_s, 1)

            def read_out(step, d, n, b):
                wait(dve, acc_s, NT * step)
                if n == 0:
                    if d == 0:
                        wait(dve, pP_full, PIECES * (b - 1) + POSTF + NH)
                    else:
                        wait(dve, F2_full, (DOWN + NE) * (b - 1) + POSTB + NH)
                for i in range(NT):
                    if i % 2 == 0:
                        dve.wait_ge(pH_full, 2 * step + 1 + i // 2)
                    dst, src = acc[d][:, i, :], psH[:, i * E:i * E + E]
                    c = cc[d][:, i, n:n + 1]
                    if n == 0:
                        w.tensor_scalar(dst, src, c, None, ALU.mult).then_inc(acc_s, 1)
                    else:
                        w.scalar_tensor_tensor(dst, src, c, dst, ALU.mult, ALU.add).then_inc(acc_s, 1)

            def statistics(x_, st_, stat_, sig, q):
                for i in range(NT):
                    w.bn_stats(st_[:, i, :], x_[:, i, :]).then_inc(sig, 1)
                dve.wait_ge(sig, q + 4)
                w.tensor_tensor(stat_[:, :, 0:2], st_[:, :, 1:3], st_[:, :, 4:6], ALU.add).then_inc(sig, 1)
                w.tensor_tensor(stat_[:, :, 4:5], st_[:, :, 1:2], st_[:, :, 4:5], ALU.subtract).then_inc(sig, 1)
                dve.wait_ge(sig, q + 6)
                w.tensor_scalar(stat_[:, :, 2:3], stat_[:, :, 0:1], 0.5, None, ALU.mult).then_inc(sig, 1)
                w.scalar_tensor_tensor(stat_[:, :, 5:6], stat_[:, :, 4:5], D / 4.0, stat_[:, :, 4:5],
                                       ALU.mult, ALU.mult).then_inc(sig, 1)
                dve.wait_ge(sig, q + 8)
                w.tensor_tensor(stat_[:, :, 1:2], stat_[:, :, 1:2], stat_[:, :, 5:6], ALU.add).then_inc(sig, 1)
                dve.wait_ge(sig, q + 9)
                w.tensor_scalar(stat_[:, :, 3:4], stat_[:, :, 1:2], 1.0 / D, EPS, ALU.mult, ALU.add).then_inc(sig, 1)

            def normalize(dst, x_, stat_, rstd_, sig):
                for i in range(NT):
                    w.tensor_scalar(dst[:, i, :], x_[:, i, :], stat_[:, i, 2:3], rstd_[:, i:i + 1],
                                    ALU.subtract, ALU.mult).then_inc(sig, 1)

            def norms(b, slot):
                if slot == LN_SLOT:
                    dve.wait_ge(x_in, 16 * b + 16)
                    wait(dve, zA, 8 * b)
                    statistics(x, st, stat, lnA, 20 * b)
                if slot == LN_SLOT + 2:
                    dve.wait_ge(rstdA, 2 * b + 1)
                    wait(dve, rN_s, 2 * b)
                    normalize(z1, x, stat, rstd, zA)
                if slot == LN_SLOT + 4:
                    dve.wait_ge(h1_s, 2 * b + 2)
                    dve.wait_ge(zA, 8 * b + 4)
                    statistics(z1, st, stat, lnA, 20 * b + 10)
                if slot == LN_SLOT + 6:
                    dve.wait_ge(rstdA, 2 * b + 2)
                    normalize(xn, z1, stat, rstd, zA)

            def silu(b, d, kind, half):
                k = 8 * b + 4 * d + kind + half
                dve.wait_ge(th_s, k + 1)
                wait(dve, yg_s[d], NH * (b - 1) + half + 1)
                dst = (u if kind == U else zs)[d][:, half, :]
                w.scalar_tensor_tensor(dst, th[:, kind + half, :], 1.0, xh[:, kind + half, :], ALU.add, ALU.mult).then_inc(silu_s, 1)

            def prep(b, d, k):
                if k - U_AT in (2, 3):
                    silu(b, d, U, k - U_AT - 2)
                if k == DT_AT + 3:
                    dve.wait_ge(sp_s, 5 * (2 * b + d) + 5)
                    w.scalar_tensor_tensor(dt_[d][:, :, :], xb[:, :, :], 0.0, ab[:, :, :], ALU.max, ALU.add)\
                        .then_inc(dt_s, 1)
                if k - Z_AT in (2, 3):
                    silu(b, d, Z, k - Z_AT - 2)

            def skip_add(b, d, half):
                if d == 0:
                    dve.wait_ge(pP_full, PIECES * b + POSTF + half + 1)
                    src, sig = psP, pP_free
                else:
                    dve.wait_ge(F2_full, (DOWN + NE) * b + POSTB + half + 1)
                    src, sig = F2, F2_free
                wait(dve, yg_s[d], NH * b + half)
                w.scalar_tensor_tensor(yt[d][:, :], u[d][:, half, :], skip[d][:, half:half + 1], src[:, :],
                                       ALU.mult, ALU.add).then_inc(sig, 1)

            def gate(fb):
                q = GATES * fb
                dve.wait_ge(F2_full, (DOWN + NE) * fb + GATE + 1)
                w.tensor_copy(gl[:, :, :], F2[:, 0:NT * NX]).then_inc(F2_free, 1)
                dve.wait_ge(F2_free, (DOWN + 1) * fb + GATE + 1)
                w.tensor_copy(gl2[:, :, :], gl[:, :, :]).then_inc(gate_s, 1)
                for i in range(NT):
                    w.max(top[:, i, :], gl[:, i, :]).then_inc(gate_s, 1)
                dve.wait_ge(gate_s, q + 5)
                w.tensor_tensor(gd[:, :], top[:, :, 1], top[:, :, 0], ALU.subtract).then_inc(gate_s, 1)
                for i in range(NT):
                    w.max_index(topi[:, i, :], top[:, i, :], gl2[:, i, :]).then_inc(gate_s, 1)
                dve.wait_ge(gate_s, q + 10)
                w.tensor_copy(topf[:, :, :], topi[:, :, 0:2]).then_inc(gate_s, 1)
                dve.wait_ge(gate_s, q + 11)
                for j in range(2):
                    w.tensor_tensor(hot[:, j, :, :], iota8[:, :].unsqueeze(1).broadcast_to([P, NT, NX]),
                                    topf[:, :, j:j + 1].broadcast_to([P, NT, NX]), ALU.is_equal).then_inc(gate_s, 1)

            def gate_weights(fb):
                q = 6 * fb
                dve.wait_ge(ge_s, fb + 1)
                w.tensor_scalar(gs[:, :], ge[:, :], 1.0, None, ALU.add).then_inc(gw_s, 1)
                dve.wait_ge(gw_s, q + 1)
                w.reciprocal(gw[:, 0, :], gs[:, :]).then_inc(gw_s, 1)
                dve.wait_ge(gw_s, q + 2)
                w.tensor_tensor(gw[:, 1, :], gw[:, 0, :], ge[:, :], ALU.mult).then_inc(gw_s, 1)
                dve.wait_ge(gate_s, GATES * fb + GATES)
                dve.wait_ge(gw_s, q + 3)
                for j in range(2):
                    w.tensor_tensor(hotw[:, j, :, :], hot[:, j, :, :],
                                    gw[:, j, :].unsqueeze(2).broadcast_to([P, NT, NX]), ALU.mult).then_inc(gw_s, 1)
                dve.wait_ge(gw_s, q + 5)
                wait(dve, facc_s, NX * NT * fb)
                w.tensor_tensor(wts[:, :, :], hotw[:, 0, :, :], hotw[:, 1, :, :], ALU.add).then_inc(gw_s, 1)

            def expert_silu(fb, slot):
                k = up_at(slot - 1)
                if k is not None:
                    at = 2 * NE * fb + k
                    dve.wait_ge(F0_free, 2 * at + 2)
                    wait(dve, act_s, at - 1)
                    w.scalar_tensor_tensor(pf[:, k % 2, :], tf[:, k % 2, :], 1.0, hf[:, k % 2, :],
                                           ALU.add, ALU.mult).then_inc(pf_s, 1)

            def ffn_side(fb, slot):
                if slot - POSTB_SLOT in (0, 1):
                    skip_add(fb, 1, slot - POSTB_SLOT)
                if slot == FX_SLOT:
                    dve.wait_ge(F2_full, (DOWN + NE) * fb + PROJ + 1)
                    dve.wait_ge(modF_in, 16 * fb + 16)
                    wait(dve, o_s, 2 * fb)
                    w.tensor_tensor(fx[:, :, :], F2[:, :].rearrange("p (k c) -> p k c", c=D),
                                    modF[:, 0, :].unsqueeze(1).broadcast_to([P, NT, D]), ALU.mult).then_inc(F2_free, 1)
                if slot == LN3_SLOT:
                    dve.wait_ge(x2_s, fb + 1)
                    wait(dve, zF_s, NT * fb)
                    statistics(x2, stF, statF, lnF, 10 * fb)
                if slot == LN3_SLOT + 1:
                    dve.wait_ge(rstdF_s, fb + 1)
                    wait(dve, F2_full, (DOWN + NE) * fb)
                    normalize(zF, x2, statF, rstdF, zF_s)
                if slot == GATE_SLOT + 1:
                    gate(fb)
                if slot == GATE_SLOT + 3:
                    gate_weights(fb)
                e = down_at(slot - 1)
                if e:
                    dve.wait_ge(F2_full, (DOWN + NE) * fb + DOWN + e + 1)
                    if e == 1:
                        dve.wait_ge(F2_free, (DOWN + 1) * fb + DOWN + 1)
                        dve.wait_ge(gw_s, 6 * fb + 6)
                    wait(dve, facc_s, NX * NT * fb + NT * (e - 1))
                    for i in range(NT):
                        w.scalar_tensor_tensor(facc[:, i, :], F2[:, i * D:i * D + D],
                                               wts[:, i, ORDER[e]:ORDER[e] + 1], facc[:, i, :],
                                               ALU.mult, ALU.add).then_inc(facc_s, 1)

            def side(b, slot, prep_b, prep_f, post_f):
                if post_f and slot - POST_F_SLOT in (1, 2):
                    skip_add(b, 0, slot - POST_F_SLOT - 1)
                if prep_f is not None:
                    norms(prep_f, slot)
                    prep(prep_f, 0, slot - PREP_SLOT[0])
                if prep_b:
                    prep(b, 1, slot - PREP_SLOT[1])

            for slot in range(STEPS):
                side(-1, slot, False, 0, False)
            dve.wait_ge(const_ok, CONSTS)

            def body(b, scan_, ffn, last):
                for slot in range(STEPS):
                    step = STEPS * b + slot
                    if scan_:
                        scan(step, slot // N, slot % N, 2 * b + 1 + slot // N)
                    if ffn:
                        expert_silu(b - 1, slot)
                    if slot > 0 and scan_:
                        read_out(step - 1, (slot - 1) // N, (slot - 1) % N, b)
                    elif slot == 0 and ffn:
                        read_out(step - 1, 1, N - 1, b - 1)
                    if scan_:
                        side(b, slot, True, None if last else b + 1, True)
                    if ffn:
                        ffn_side(b - 1, slot)

            passes(dve, body)

        @block.tensor
        def _(pe):
            m = nc.tensor
            pe.wait_ge(ident_ok, 2)
            pe.wait_ge(loaded, LOADS)
            for d in range(2):
                pe.wait_ge(taps_ok, NH * TAPS * (d + 1))
                if d:
                    pe.wait_ge(wt_ev, 5)
                for half in range(NH):
                    for j in range(TAPS):
                        col = (half * TAPS + j) * P
                        m.transpose(psA[:, col:col + P], win_tap[d][:, half, j, :], ident[:, :])
                    m.transpose(psH[:, half * P:half * P + P], win_nat[d][:, NH + half, :], ident[:, :])
                    k = R + 2 * N
                    m.transpose(psH[:, (2 + half) * P:(2 + half) * P + k], wx_nat[d][:, half * P:half * P + P],
                                ident[0:k, 0:k])
                    m.transpose(psH[0:R, (4 + half) * P:(5 + half) * P], wdt_nat[d][:, half, :], ident[:, :])
                    last = m.transpose(psH[:, (6 + half) * P:(7 + half) * P], wout_nat[d][:, half * P:half * P + P],
                                       ident[:, :])
                last.then_inc(wt_tr, 1)
            pe.wait_ge(c_step, 2)
            m.transpose(F0[:, 0:NB], c_silu[:, :], ident[0:NB, 0:NB]).then_inc(c_step, 1)
            pe.wait_ge(c_step, 4)
            m.matmul(F0[0:NB, :], cT[:, :], wmod[:, 0:T], start=True, stop=True)
            m.matmul(F1[0:NB, 0:2 * D], cT[:, :], wmod[:, T:KINDS * D], start=True, stop=True).then_inc(mod_mm, 1)
            pe.wait_ge(mod_v, KINDS)
            pe.wait_ge(wt_ev, 10)
            pe.wait_ge(halved, 7)

            def tr_h(step, n):
                pe.wait_ge(h_s, step + 1)
                for i in range(NT):
                    if i % 2 == 0:
                        wait(pe, acc_s, NT * step - NT + i + 2)
                    for half in range(NH):
                        last = m.transpose(psH[:, i * E + half * P:i * E + half * P + P],
                                           h[:, n % 2, half, i * P:i * P + P], ident[:, :])
                    if i % 2 == 1:
                        last.then_inc(pH_full, 1)

            def prep(b, d, k):
                def open_piece(kind, half=0):
                    wait(pe, pP_free, PIECES * b + piece(d, kind, half))
                if k - U_AT in (0, 1):
                    k -= U_AT
                    open_piece(U, k)
                    for j in range(TAPS):
                        lo = j if d == 0 else 2 * PAD - j
                        last = m.matmul(psP[:, :], wcT[d][:, k, j, :], xnT[:, lo:lo + T],
                                        start=(j == 0), stop=(j == TAPS - 1))
                    last.then_inc(pP_full, 1)
                    return
                if k == XD_AT:
                    pe.wait_ge(silu_s, 8 * b + 4 * d + 2)
                    open_piece(XD)
                    for half in range(NH):
                        last = m.matmul(psP[0:R + N, :], wxT[d][:, half, 0:R + N], u[d][:, half, :],
                                        start=(half == 0), stop=(half == NH - 1))
                    last.then_inc(pP_full, 1)
                if k == CP_AT:
                    open_piece(CP)
                    for i in range(NT):
                        for half in range(NH):
                            last = m.matmul(psP[:, i * N:(i + 1) * N], u[d][:, half, i * P:i * P + P],
                                            wxT[d][:, half, R + N:R + 2 * N], start=(half == 0), stop=(half == NH - 1))
                    last.then_inc(pP_full, 1)
                if k - DT_AT in (0, 1):
                    open_piece(DT, k - DT_AT)
                    m.matmul(psP[:, :], wdtT[d][:, k - DT_AT, :], xd[0:R, :], start=True, stop=True).then_inc(pP_full, 1)
                if k - Z_AT in (0, 1):
                    open_piece(Z, k - Z_AT)
                    m.matmul(psP[:, :], wzT[d][:, k - Z_AT, :], xnT[:, PAD:PAD + T], start=True, stop=True)\
                        .then_inc(pP_full, 1)

            def side(b, slot, prep_b, prep_f, post_f):
                if post_f and slot in (POST_F_SLOT, POST_F_SLOT + 1):
                    half = slot - POST_F_SLOT
                    pe.wait_ge(acc_s, NT * (STEPS * b + N))
                    wait(pe, pP_free, PIECES * b + POSTF + half)
                    for i in range(NT):
                        last = m.transpose(psP[:, i * P:i * P + P], acc[0][:, i, half * P:half * P + P], ident[:, :])
                    last.then_inc(pP_full, 1)
                if prep_f is not None:
                    if slot == XN_SLOT:
                        pe.wait_ge(zA, 8 * prep_f + 8)
                        wait(pe, pP_free, PIECES * prep_f)
                        for i in range(NT):
                            last = m.transpose(psP[:, i * P:i * P + P], xn[:, i, :], ident[:, :])
                        last.then_inc(pP_full, 1)
                    prep(prep_f, 0, slot - PREP_SLOT[0])
                if prep_b:
                    prep(b, 1, slot - PREP_SLOT[1])

            def ffn_side(fb, slot):
                free = (DOWN + 1) * fb
                if slot - POSTB_SLOT in (0, 1):
                    half = slot - POSTB_SLOT
                    if half == 0:
                        pe.wait_ge(acc_s, NT * (STEPS * fb + STEPS))
                        wait(pe, facc_s, NX * NT * fb)
                    else:
                        pe.wait_ge(F2_free, free + POSTB + half)
                    for i in range(NT):
                        last = m.transpose(F2[:, i * P:i * P + P], acc[1][:, i, half * P:half * P + P], ident[:, :])
                    last.then_inc(F2_full, 1)
                k = up_at(slot)
                if k is not None:
                    x_, half = ORDER[k // 2], k % 2
                    at = 2 * NE * fb + k
                    if k == 0:
                        pe.wait_ge(F2_free, free + H2T + 1)
                    wait(pe, F0_free, 2 * at)
                    m.matmul(F0[:, :], w1[:, x_, half * P:half * P + P], h2T[:, :], start=True, stop=True)\
                        .then_inc(F0_full, 1)
                    wait(pe, F1_free, at)
                    m.matmul(F1[:, :], w2[:, x_, half * P:half * P + P], h2T[:, :], start=True, stop=True)\
                        .then_inc(F1_full, 1)

            def ffn_late(fb, slot):
                free = (DOWN + 1) * fb
                if slot - PROJ_SLOT in (0, 1):
                    if slot == PROJ_SLOT:
                        for d in range(2):
                            pe.wait_ge(yg_s[d], NH * fb + NH)
                        pe.wait_ge(F2_free, free + PROJ)
                    for i in (0, 1) if slot == PROJ_SLOT else (2, 3):
                        for k in range(2 * NH):
                            last = m.matmul(F2[:, i * D:i * D + D], yg[k // NH][:, k % NH, i * P:i * P + P],
                                            woutT[k // NH][:, k % NH, :], start=(k == 0), stop=(k == 2 * NH - 1))
                    if slot == PROJ_SLOT + 1:
                        last.then_inc(F2_full, 1)
                if slot == H2T_SLOT:
                    pe.wait_ge(h2_s, 2 * fb + 2)
                    pe.wait_ge(F2_free, free + H2T)
                    for i in range(NT):
                        last = m.transpose(F2[:, i * P:i * P + P], zF[:, i, :], ident[:, :])
                    last.then_inc(F2_full, 1)
                if slot == GATE_SLOT:
                    pe.wait_ge(F2_free, free + GATE)
                    for i in range(NT):
                        last = m.matmul(F2[:, i * NX:(i + 1) * NX], h2T[:, i * P:i * P + P], gate_w[:, :],
                                        start=True, stop=True)
                    last.then_inc(F2_full, 1)
                e = down_at(slot)
                if e is not None:
                    pe.wait_ge(act_s, 2 * NE * fb + 2 * e + 2)
                    if e <= 1:
                        pe.wait_ge(F2_free, free + DOWN + e)
                    else:
                        pe.wait_ge(facc_s, NX * NT * fb + NT * (e - 1))
                    for i in range(NT):
                        for half in range(2):
                            last = m.matmul(F2[:, i * D:i * D + D], act[:, e % 2, half, i * P:i * P + P],
                                            w3[:, ORDER[e], half, :], start=(half == 0), stop=(half == 1))
                    last.then_inc(F2_full, 1)

            for slot in range(STEPS):
                side(-1, slot, False, 0, False)

            def body(b, scan_, ffn, last):
                for slot in range(STEPS):
                    step = STEPS * b + slot
                    if (slot > 0 and scan_) or (slot == 0 and ffn):
                        tr_h(step - 1, (slot - 1) % N)
                    if ffn:
                        ffn_side(b - 1, slot)
                        ffn_late(b - 1, slot)
                    if scan_:
                        side(b, slot, True, None if last else b + 1, True)

            passes(pe, body)


_NAMES = {
    "L0_attn_x": "x", "L0_attn_norm_g": "norm_g", "L0_attn_norm_b": "norm_b", "L0_ffn_gate_w": "gate_w",
    "L0_ffn_ew1": "ew1", "L0_ffn_ew2": "ew2", "L0_ffn_ew3": "ew3", "L0_ffn_sw1": "sw1", "L0_ffn_sw2": "sw2",
    "L0_ffn_sw3": "sw3", "L0_c": "c", "L0_wmod": "wmod",
}
_DIR = ["Win", "convw", "convb", "Wx", "Wdt", "bdt", "Alog", "D", "Wout"]


def kernel(**inputs):
    import numpy as _np
    import concourse.bacc as _bacc
    from concourse import mybir as _mybir
    from concourse.bass_utils import run_bass_kernel_spmd as _run

    nc = _bacc.Bacc("TRN2", target_bir_lowering=False, num_devices=1)
    arrays = {}

    def given(name):
        arr = _np.ascontiguousarray(inputs[name])
        arrays[f"in_{name}"] = arr
        return nc.dram_tensor(f"in_{name}", arr.shape, _mybir.dt.from_np(arr.dtype), kind="ExternalInput").ap()

    t = {short: given(name) for name, short in _NAMES.items()}
    for d in "fb":
        t[d] = {w: given(f"L0_attn_{d}_{w}") for w in _DIR}
    out = nc.dram_tensor("out_x", (NB, T, D), _mybir.dt.float32, kind="ExternalOutput").ap()
    adaln_mamba_moe(nc, t, out)
    r = _run(nc, [arrays], core_ids=[0])
    return r.results[0]["out_x"]
```

```python
import concourse.bass as bass
from concourse import mybir
from contextlib import ExitStack

NB, T, D = 16, 512, 128
P = 128
NT = T // P
E = 2 * D
NH = E // P
N = 16
R = 8
TAPS = 4
NX = 8
NE = NX + 1
HID = 2 * D
EPS = 1e-5
STEPS = 2 * N
PAD = TAPS - 1
KINDS = 6

U, Z, XD, DT, CP = 0, 2, 4, 5, 7
PREP = 8
PIECES = 1 + 2 * PREP + NH
POSTB, PROJ, H2T, GATE, DOWN = 0, 2, 3, 4, 5

PREP_SLOT = (19, 0)
U_AT, Z_AT, XD_AT, DT_AT, LN1P_AT, CP_AT, V_AT = 0, 4, 6, 7, 9, 9, 11
LN_SLOT, XN_SLOT = 9, 16
POST_F_SLOT = 17
POSTB_SLOT, PROJ_SLOT, FX_SLOT, LN3_SLOT, H2T_SLOT, GATE_SLOT = 1, 3, 5, 6, 8, 9
UP_SLOTS = [slot for slot in range(9, 28) if slot not in (22,)]
DOWN_SLOTS = [slot for slot in range(12, 32) if slot not in (19, 21)]


def piece(d, kind, half=0):
    return 1 + PREP * d + kind + half


def xn_piece(b):
    return 0 if isinstance(b, int) and b == 0 else PIECES * b - NH


def post_piece(b, half):
    no_xn = 1 if isinstance(b, int) and b == NB - 1 else 0
    return PIECES * b + PIECES - 1 + half - no_xn


def up_at(slot):
    return UP_SLOTS.index(slot) if slot in UP_SLOTS else None


def down_at(slot):
    return divmod(DOWN_SLOTS.index(slot), 2) if slot in DOWN_SLOTS else None


ORDER = [NX] + list(range(NX))


def adaln_mamba_moe(nc, t, out):
    f32, u32 = mybir.dt.float32, mybir.dt.uint32
    ALU, ACT = mybir.AluOpType, mybir.ActivationFunctionType
    ctx = ExitStack()
    with ctx:
        def sb(name, shape, dt=f32):
            return ctx.enter_context(nc.sbuf_tensor(name, shape, dt))

        def ps(name, shape):
            return ctx.enter_context(nc.psum_tensor(name, shape, f32))

        def sem(name):
            return ctx.enter_context(nc.semaphore(name))

        ident = sb("ident", [P, P])
        iota8 = sb("iota8", [P, NX])
        wdt_nat = [sb(f"wdt_nat{d}", [P, NH, R]) for d in range(2)]
        convw = [sb(f"convw{d}", [P, NH, TAPS]) for d in range(2)]
        convb = [sb(f"convb{d}", [P, NH]) for d in range(2)]
        bdt = [sb(f"bdt{d}", [P, NH]) for d in range(2)]
        skip = [sb(f"skip{d}", [P, NH]) for d in range(2)]
        alog = [sb(f"alog{d}", [P, NH, N]) for d in range(2)]
        aneg = [sb(f"aneg{d}", [P, NH, N]) for d in range(2)]
        wcT = [sb(f"wcT{d}", [D, NH, TAPS, P]) for d in range(2)]
        wzT = [sb(f"wzT{d}", [D, NH, P]) for d in range(2)]
        wxT = [sb(f"wxT{d}", [P, NH, R + 2 * N]) for d in range(2)]
        wdtT = [sb(f"wdtT{d}", [R, NH, P]) for d in range(2)]
        woutT = [sb(f"woutT{d}", [P, NH, D]) for d in range(2)]
        norm = sb("norm", [P, 2])
        gate_w = sb("gate_w", [D, NX])
        w1 = sb("w1", [D, NE, HID])
        w2 = sb("w2", [D, NE, HID])
        w3 = sb("w3", [P, NE, 2, D])
        c_nat = sb("c_nat", [NB, D])
        c_th = sb("c_th", [NB, D])
        c_silu = sb("c_silu", [NB, D])
        cT = sb("cT", [D, NB])
        gsgn = sb("gsgn", [NB, 2, D])
        gabs = sb("gabs", [NB, 2, D])
        modA = sb("modA", [P, 2, D])
        modF = sb("modF", [P, 2, D])
        modC = sb("modC", [D, 2])
        x = sb("x", [P, NT, D])
        st = sb("st", [P, NT, 6])
        stat = sb("stat", [P, NT, 6])
        mhalf = sb("mhalf", [P, NT])
        epsilon = sb("epsilon", [P, NT])
        scales = sb("scales", [P, NT, 3])
        rstd = sb("rstd", [P, NT])
        z1 = sb("z1", [P, NT, D])
        xn = sb("xn", [P, NT, D])
        xnT = sb("xnT", [D, T + 2 * PAD])
        h1K = sb("h1K", [P, NT, D])
        xR = sb("xR", [P, NT, D])
        diag = sb("diag", [P, 2, NH, P])
        xh = sb("xh", [P, 4, T])
        th = sb("th", [P, 4, T])
        u = [sb(f"u{d}", [P, NH, T]) for d in range(2)]
        zs = [sb(f"zs{d}", [P, NH, T]) for d in range(2)]
        xd = sb("xd", [R + N, T])
        cc = [sb(f"cc{d}", [P, NT, N]) for d in range(2)]
        xb = sb("xb", [P, NH, T])
        ab = sb("ab", [P, NH, T])
        dt_ = [sb(f"dt{d}", [P, NH, T]) for d in range(2)]
        v = [sb(f"v{d}", [P, NH, T]) for d in range(2)]
        bb = sb("bb", [P, 2, 2, T])
        bt = sb("bt", [P, 2, NH, T])
        zero = sb("zero", [P, NH, 1])
        h = sb("h", [P, 2, NH, T])
        acc = [sb(f"acc{d}", [P, NT, E]) for d in range(2)]
        def part(buf, rows, lo, shape):
            flat = buf.rearrange("p a b c -> p (a b c)") if len(buf.shape) == 4 else buf.rearrange("p a b -> p (a b)")
            size = 1
            for k in shape:
                size *= k
            flat = flat[0:rows, lo:lo + size]
            if len(shape) == 1:
                return flat
            if len(shape) == 2:
                return flat.rearrange("p (a b) -> p a b", b=shape[1])
            return flat.rearrange("p (a b c) -> p a b c", b=shape[1], c=shape[2])

        win_tap = [part(bt[:, :, :, :], P, d * NH * TAPS * D, [NH, TAPS, D]) for d in range(2)]
        win_nat = [part(h[:, :, :, :], P, d * 4 * D, [4, D]) for d in range(2)]
        wx_nat = [part(h[:, :, :, :], R + 2 * N, 8 * D + d * E, [E]) for d in range(2)]
        wout_nat = [part(h[:, :, :, :], D, 12 * D + d * E, [E]) for d in range(2)]
        wmod = part(acc[0][:, :, :], D, 0, [KINDS * D])
        mod = part(acc[1][:, :, :], NB, 0, [KINDS, D])
        yg = [sb(f"yg{d}", [P, NH, T]) for d in range(2)]
        fx = sb("fx", [P, NT, D])
        x2 = sb("x2", [P, NT, D])
        stF = sb("stF", [P, NT, 6])
        statF = sb("statF", [P, NT, 6])
        rstdF = sb("rstdF", [P, NT])
        zF = sb("zF", [P, NT, D])
        h2T = sb("h2T", [D, T])
        gl = sb("gl", [P, NT, NX])
        gl2 = sb("gl2", [P, NT, NX])
        top = sb("top", [P, NT, NX])
        topi = sb("topi", [P, NT, NX], u32)
        topf = sb("topf", [P, NT, 2])
        gd = sb("gd", [P, NT])
        ge = sb("ge", [P, NT])
        gs = sb("gs", [P, NT])
        gw = sb("gw", [P, 2, NT])
        hot = sb("hot", [P, 2, NT, NX])
        hotw = sb("hotw", [P, 2, NT, NX])
        wts = sb("wts", [P, NT, NX])
        tf = sb("tf", [P, 2, T])
        hf = sb("hf", [P, 2, T])
        gf = sb("gf", [P, 3, T])
        pf = sb("pf", [P, 2, T])
        act = sb("act", [P, 3, 2, T])
        facc = sb("facc", [P, NT, D])
        osb = sb("osb", [P, NT, D])

        psA = ps("psA", [P, NH * T])
        psH = ps("psH", [P, NT * E])
        psP = ps("psP", [P, T])
        F0 = ps("F0", [P, T])
        F1 = ps("F1", [P, T])
        F2 = ps("F2", [P, T])

        b_dram = nc.dram_tensor("b_rows", (2, N, T), f32, kind="Internal").ap()
        mod_dram = nc.dram_tensor("mod_table", (NB, KINDS * D), f32, kind="Internal").ap()

        loaded = sem("loaded")
        diag_ok = sem("diag_ok")
        c_loaded = sem("c_loaded")
        const_ok = sem("const_ok")
        ident_ok = sem("ident_ok")
        taps_ok = sem("taps_ok")
        wt_tr = sem("wt_tr")
        wt_ev = sem("wt_ev")
        halved = sem("halved")
        c_step = sem("c_step")
        mod_mm = sem("mod_mm")
        mod_v = sem("mod_v")
        mod_out = sem("mod_out")
        x_in = sem("x_in")
        modA_in = sem("modA_in")
        xR_in = sem("xR_in")
        lnA = sem("lnA")
        rstdA = sem("rstdA")
        zA = sem("zA")
        h1_s = sem("h1_s")
        h1K_s = sem("h1K_s")
        pP_full = sem("pP_full")
        pP_free = sem("pP_free")
        th_s = sem("th_s")
        silu_s = sem("silu_s")
        sp_s = sem("sp_s")
        dt_s = sem("dt_s")
        v_s = sem("v_s")
        brow_out = sem("brow_out")
        bb_in = [sem(f"bb_in{k}") for k in range(2)]
        bt_s = sem("bt_s")
        a_s = sem("a_s")
        h_s = sem("h_s")
        pH_full = sem("pH_full")
        acc_s = sem("acc_s")
        modF_in = sem("modF_in")
        F2_full = sem("F2_full")
        F2_free = sem("F2_free")
        x2_s = sem("x2_s")
        lnF = sem("lnF")
        rstdF_s = sem("rstdF_s")
        zF_s = sem("zF_s")
        gate_s = sem("gate_s")
        ge_s = sem("ge_s")
        F0_full = sem("F0_full")
        F1_full = sem("F1_full")
        F0_free = sem("F0_free")
        F1_free = sem("F1_free")
        pf_s = sem("pf_s")
        act_s = sem("act_s")
        facc_s = sem("facc_s")
        gw_s = sem("gw_s")
        wts_s = sem("wts_s")
        o_s = sem("o_s")
        out_d = sem("out_d")
        GATES = 13
        GATE_D = 6
        LOADS = 16 * 27
        MOD_STEPS = 12
        CONSTS = 9

        block = ctx.enter_context(nc.Block())

        def wait(eng, s, value):
            if not (isinstance(value, int) and value <= 0):
                eng.wait_ge(s, value)

        def passes(eng, body):
            body(0, True, False, False)
            body(1, True, True, False)
            with eng.Fori(2, NB - 1) as b:
                body(b, True, True, False)
            body(NB - 1, True, True, True)
            body(NB, False, True, True)

        @block.sync
        def _(sp):
            sp.dma_start(c_nat[:, :], t["c"]).then_inc(c_loaded, 16)
            sp.dma_start(wmod[:, :], t["wmod"]).then_inc(c_loaded, 16)
            sp.dma_start(x[:, :, :], t["x"][0:1].rearrange("a (k p) d -> p (a k) d", p=P)).then_inc(x_in, 16)
            small = nc.allow_non_contiguous_dma(reason="small weight columns")
            with small:
                for d in range(2):
                    w = t["fb"[d]]
                    for dst, src in (
                        (win_nat[d][:, :, :], w["Win"].rearrange("(k p) d -> p k d", p=P)),
                        (wx_nat[d][:, :], w["Wx"]),
                        (wdt_nat[d][:, :, :], w["Wdt"].rearrange("(k p) r -> p k r", p=P)),
                        (wout_nat[d][:, :], w["Wout"]),
                        (convw[d][:, :, :], w["convw"].rearrange("(k p) a j -> p k (a j)", p=P)),
                        (convb[d][:, :], w["convb"].rearrange("(k p) -> p k", p=P)),
                        (bdt[d][:, :], w["bdt"].rearrange("(k p) -> p k", p=P)),
                        (skip[d][:, :], w["D"].rearrange("(k p) -> p k", p=P)),
                        (alog[d][:, :, :], w["Alog"].rearrange("(k p) n -> p k n", p=P)),
                        (norm[:, d:d + 1], t["norm_g" if d == 0 else "norm_b"].rearrange("(p a) -> p a", a=1)),
                    ):
                        sp.dma_start(dst, src).then_inc(loaded, 16)
                for dst, src in (
                    (gate_w[:, :], t["gate_w"]),
                    (w1[:, 0:NX, :], t["ew1"].rearrange("e d h -> d e h")),
                    (w2[:, 0:NX, :], t["ew2"].rearrange("e d h -> d e h")),
                    (w3[:, 0:NX, :, :], t["ew3"].rearrange("e (k p) d -> p e k d", p=P)),
                    (w1[:, NX, :], t["sw1"]),
                    (w2[:, NX, :], t["sw2"]),
                    (w3[:, NX, :, :], t["sw3"].rearrange("(k p) d -> p k d", p=P)),
                ):
                    sp.dma_start(dst, src).then_inc(loaded, 16)
            sp.wait_ge(mod_v, MOD_STEPS)
            sp.dma_start(mod_dram, mod[:, :, :].rearrange("b k d -> b (k d)")).then_inc(mod_out, 16)
            sp.wait_ge(mod_out, 16)

            def load(b):
                wait(sp, h1_s, 2 * b)
                if not (isinstance(b, int) and b == 0):
                    sp.dma_start(x[:, :, :], t["x"][bass.ds(b, 1)].rearrange("a (k p) d -> p (a k) d", p=P))\
                        .then_inc(x_in, 16)
                row = mod_dram[bass.ds(b, 1), 0:2 * D].broadcast_to([P, 2 * D])
                sp.dma_start(modA[:, :, :].rearrange("p k d -> p (k d)"), row).then_inc(modA_in, 16)

            def rows_out(b, d):
                sp.wait_ge(pP_free, PIECES * b + piece(d, XD) + 1)
                sp.dma_start(b_dram[d], xd[R:R + N, :]).then_inc(brow_out, 16)

            def rows_in(b, d, pair):
                used = 2 * (N * b + N * d // 2 + pair - 1)
                if pair == 0:
                    sp.wait_ge(brow_out, 16 * (2 * b + d + 1))
                wait(sp, bt_s, used)
                src = b_dram[d, 2 * pair:2 * pair + 2, :].rearrange("n t -> (n t)").unsqueeze(0)
                sp.dma_start(bb[:, pair % 2, :, :].rearrange("p n t -> p (n t)"), src.broadcast_to([P, 2 * T]))\
                    .then_inc(bb_in[pair % 2], 16)

            load(0)
            rows_out(0, 0)
            rows_in(0, 0, 0)
            rows_in(0, 0, 1)

            def body(b, scan, ffn, last):
                for slot in range(STEPS):
                    if scan and slot == PREP_SLOT[1] + XD_AT + 1:
                        rows_out(b, 1)
                    if scan and not last and slot == PREP_SLOT[0] + XD_AT + 1:
                        rows_out(b + 1, 0)
                    if slot % 2 == 0:
                        step = slot + 4
                        if scan and step < STEPS:
                            rows_in(b, step // N, step % N // 2)
                        elif scan and not last:
                            rows_in(b + 1, 0, (step - STEPS) // 2)
                    if slot == 0:
                        early(b, scan, ffn, last)
                    if slot == 0 and not (isinstance(b, int) and b < 2):
                        store(b - 2)

            def early(b, scan, ffn, last):
                if ffn:
                    fb = b - 1
                    wait(sp, o_s, 2 * fb)
                    for k, kind in enumerate((2, 5)):
                        row = mod_dram[bass.ds(fb, 1), kind * D:kind * D + D].broadcast_to([P, D])
                        sp.dma_start(modF[:, k, :], row).then_inc(modF_in, 16)
                    with nc.allow_non_contiguous_dma(reason="two columns"):
                        sp.dma_start(modC[:, :], mod_dram[bass.ds(fb, 1), 3 * D:5 * D]
                                     .rearrange("a (k p) -> p (a k)", p=P)).then_inc(modF_in, 16)
                    sp.dma_start(xR[:, :, :], t["x"][bass.ds(fb, 1)].rearrange("a (k p) d -> p (a k) d", p=P))\
                        .then_inc(xR_in, 16)
                if scan and not last:
                    load(b + 1)

            def store(fb):
                sp.wait_ge(o_s, 2 * fb + 2)
                sp.dma_start(out[bass.ds(fb, 1)].rearrange("a (k p) d -> p (a k) d", p=P), osb[:, :, :])\
                    .then_inc(out_d, 16)

            passes(sp, body)
            store(NB - 1)
            sp.wait_ge(out_d, 16 * NB)

        @block.gpsimd
        def _(pool):
            g = nc.gpsimd
            g.memset(ident[:, :], 0.0).then_inc(ident_ok, 1)
            pool.wait_ge(ident_ok, 1)
            g.affine_select(out=ident[:, :], in_=ident[:, :], compare_op=ALU.not_equal, fill=1.0, base=0,
                            pattern=[[-1, P]], channel_multiplier=1).then_inc(ident_ok, 1)
            g.iota(iota8[:, :], pattern=[[1, NX]], base=0, channel_multiplier=0,
                   allow_small_or_imprecise_dtypes=True).then_inc(const_ok, 1)
            g.memset(mhalf[:, :], -0.5).then_inc(const_ok, 1)
            g.memset(epsilon[:, :], EPS).then_inc(const_ok, 1)
            for k, scale in enumerate((0.5, 1.0 / D, 0.5)):
                g.memset(scales[:, :, k:k + 1], scale).then_inc(const_ok, 1)

            def over_tiles(row):
                return row.unsqueeze(1).broadcast_to([P, NT, D])

            def bmul(step, d, n):
                wait(pool, h_s, step - 1)
                if n == 0:
                    pool.wait_ge(v_s, bmul.unit)
                if n % 2 == 0:
                    pool.wait_ge(bb_in[n // 2 % 2], 64 * bmul.unit + 16 * (n // 4) - 48)
                g.tensor_tensor(bt[:, n % 2, :, :], v[d][:, :, :],
                                bb[:, n // 2 % 2, n % 2, :].unsqueeze(1).broadcast_to([P, NH, T]),
                                ALU.mult).then_inc(bt_s, 1)

            def moments(st_, stat_, rstd_, sig, q):
                g.tensor_tensor(stat_[:, :, 0:2], st_[:, :, 1:3], st_[:, :, 4:6], ALU.add).then_inc(sig, 1)
                g.tensor_tensor(stat_[:, :, 2:3], st_[:, :, 1:2], st_[:, :, 4:5], ALU.subtract).then_inc(sig, 1)
                pool.wait_ge(sig, q + 2)
                g.tensor_tensor(stat_[:, :, 0:3], stat_[:, :, 0:3], scales[:, :, :], ALU.mult).then_inc(sig, 1)
                pool.wait_ge(sig, q + 3)
                g.tensor_tensor(stat_[:, :, 3:4], stat_[:, :, 2:3], stat_[:, :, 2:3], ALU.mult).then_inc(sig, 1)
                pool.wait_ge(sig, q + 4)
                g.tensor_tensor(stat_[:, :, 4:5], stat_[:, :, 1:2], stat_[:, :, 3:4], ALU.add).then_inc(sig, 1)
                pool.wait_ge(sig, q + 5)
                g.tensor_tensor(stat_[:, :, 5], stat_[:, :, 4], epsilon[:, :], ALU.add).then_inc(sig, 1)
                pool.wait_ge(sig, q + 6)
                g.tensor_tensor(rstd_[:, :], stat_[:, :, 5], mhalf[:, :], ALU.pow).then_inc(sig, 1)

            def norms(b, slot):
                if slot == LN_SLOT + 1:
                    if isinstance(b, int) and b == 0:
                        pool.wait_ge(const_ok, CONSTS)
                    pool.wait_ge(lnA, 8 * b + 4)
                    wait(pool, zA, 8 * b)
                    moments(st, stat, rstd, rstdA, 14 * b)
                if slot == LN_SLOT + 3:
                    pool.wait_ge(zA, 8 * b + 4)
                    pool.wait_ge(modA_in, 16 * b + 16)
                    wait(pool, pP_full, xn_piece(b - 1) + 1)
                    g.tensor_tensor(xn[:, :, :], z1[:, :, :], over_tiles(modA[:, 1, :]), ALU.mult).then_inc(h1_s, 1)
                    pool.wait_ge(h1_s, 2 * b + 1)
                    g.tensor_tensor(z1[:, :, :], xn[:, :, :], over_tiles(modA[:, 0, :]), ALU.add).then_inc(h1_s, 1)
                if slot == LN_SLOT + 5:
                    pool.wait_ge(lnA, 8 * b + 8)
                    moments(st, stat, rstd, rstdA, 14 * b + 7)

            def make_dt(b, d):
                pool.wait_ge(pP_free, PIECES * b + piece(d, DT, 1) + 1)
                pool.wait_ge(sp_s, 5 * (2 * b + d) + 5)
                g.tensor_tensor(dt_[d][:, :, :], xb[:, :, :], ab[:, :, :], ALU.add).then_inc(dt_s, 1)

            def make_v(b, d):
                pool.wait_ge(dt_s, 2 * b + d + 1)
                wait(pool, bt_s, STEPS * (b - 1) + N * (d + 1))
                g.tensor_tensor(v[d][:, :, :], u[d][:, :, :], dt_[d][:, :, :], ALU.mult).then_inc(v_s, 1)

            def output(fb):
                pool.wait_ge(facc_s, NX * NT * fb + NX * NT)
                g.tensor_tensor(fx[:, :, :], facc[:, :, :], over_tiles(modF[:, 1, :]), ALU.mult).then_inc(o_s, 1)
                pool.wait_ge(o_s, 2 * fb + 1)
                wait(pool, out_d, 16 * fb)
                g.tensor_tensor(osb[:, :, :], fx[:, :, :], x2[:, :, :], ALU.add).then_inc(o_s, 1)

            def expert_weights(fb):
                q = 3 * fb
                pool.wait_ge(gate_s, GATES * fb + GATES)
                pool.wait_ge(gw_s, 3 * fb + 3)
                for j in range(2):
                    g.tensor_tensor(hotw[:, j, :, :], hot[:, j, :, :],
                                    gw[:, j, :].unsqueeze(2).broadcast_to([P, NT, NX]), ALU.mult).then_inc(wts_s, 1)
                pool.wait_ge(wts_s, q + 2)
                wait(pool, facc_s, NX * NT * fb)
                g.tensor_tensor(wts[:, :, :], hotw[:, 0, :, :], hotw[:, 1, :, :], ALU.add).then_inc(wts_s, 1)

            def ffn_side(fb, slot):
                if slot == GATE_SLOT + 4:
                    expert_weights(fb)
                if slot == FX_SLOT:
                    pool.wait_ge(F2_free, (DOWN + 1) * fb + PROJ + 1)
                    pool.wait_ge(modF_in, 48 * fb + 48)
                    wait(pool, o_s, 2 * fb)
                    g.tensor_tensor(x2[:, :, :], fx[:, :, :], over_tiles(modF[:, 0, :]), ALU.mult).then_inc(x2_s, 1)
                    pool.wait_ge(x2_s, 2 * fb + 1)
                    pool.wait_ge(xR_in, 16 * fb + 16)
                    g.tensor_tensor(x2[:, :, :], x2[:, :, :], xR[:, :, :], ALU.add).then_inc(x2_s, 1)
                if slot == LN3_SLOT:
                    pool.wait_ge(lnF, NT * fb + NT)
                    wait(pool, zF_s, NT * fb)
                    moments(stF, statF, rstdF, rstdF_s, 7 * fb)
                k = up_at(slot - 1)
                if k is not None:
                    at = 2 * NE * fb + k
                    pool.wait_ge(pf_s, at + 1)
                    pool.wait_ge(F1_free, at + 1)
                    wait(pool, F2_full, (DOWN + NE) * fb + DOWN + k // 2 - 2 if k >= 6 else (DOWN + NE) * fb)
                    g.tensor_tensor(act[:, k // 2 % 3, k % 2, :], pf[:, k % 2, :], gf[:, k % 3, :], ALU.mult)\
                        .then_inc(act_s, 1)

            def side(b, slot, prep_b, prep_f, post_f):
                if prep_f is not None:
                    norms(prep_f, slot)
                    if slot == PREP_SLOT[0] + DT_AT + 3:
                        make_dt(prep_f, 0)
                    if slot == PREP_SLOT[0] + V_AT:
                        make_v(prep_f, 0)
                if prep_b and slot == PREP_SLOT[1] + DT_AT + 3:
                    make_dt(b, 1)
                if prep_b and slot == PREP_SLOT[1] + V_AT:
                    make_v(b, 1)

            for slot in range(STEPS):
                side(-1, slot, False, 0, False)
            bmul.unit = 1
            bmul(0, 0, 0)

            def body(b, scan, ffn, last):
                for slot in range(STEPS):
                    if scan:
                        nxt = slot + 1
                        if nxt < STEPS:
                            bmul.unit = 2 * b + 1 + nxt // N
                            bmul(STEPS * b + nxt, nxt // N, nxt % N)
                        elif not last:
                            bmul.unit = 2 * b + 3
                            bmul(STEPS * b + nxt, 0, 0)
                    if slot == 0 and not (isinstance(b, int) and b < 2):
                        output(b - 2)
                    if scan:
                        side(b, slot, True, None if last else b + 1, True)
                    if ffn:
                        ffn_side(b - 1, slot)

            passes(pool, body)
            output(NB - 1)

        @block.scalar
        def _(act_e):
            s = nc.scalar
            act_e.wait_ge(c_loaded, 32)
            s.activation(c_th[:, :], c_nat[:, :], ACT.Tanh, scale=0.5).then_inc(c_step, 1)
            act_e.wait_ge(c_step, 3)
            s.activation(cT[:, :], F0[:, 0:NB], ACT.Copy).then_inc(c_step, 1)
            act_e.wait_ge(loaded, LOADS)
            for d in range(2):
                s.activation(aneg[d][:, :, :], alog[d][:, :, :], ACT.Exp).then_inc(halved, 1)
            act_e.wait_ge(halved, 2)
            for d in range(2):
                s.activation(aneg[d][:, :, :], aneg[d][:, :, :], ACT.Copy, scale=-1.0).then_inc(halved, 1)
                s.activation(convb[d][:, :], convb[d][:, :], ACT.Copy, scale=0.5).then_inc(halved, 1)
            s.activation(w3[:, :, :, :], w3[:, :, :, :], ACT.Copy, scale=0.5).then_inc(halved, 1)
            for d in range(2):
                act_e.wait_ge(wt_tr, d + 1)
                s.activation(wcT[d][:, :, :, :], psA[:, 0:NH * TAPS * P], ACT.Copy).then_inc(wt_ev, 1)
                s.activation(wzT[d][:, :, :], psH[:, 0:NH * P], ACT.Copy).then_inc(wt_ev, 1)
                s.activation(wxT[d][:, :, :], psH[:, 2 * P:4 * P].rearrange("p (k c) -> p k c", c=P)[:, :, 0:R + 2 * N],
                             ACT.Copy).then_inc(wt_ev, 1)
                s.activation(wdtT[d][:, :, :], psH[0:R, 4 * P:6 * P], ACT.Copy).then_inc(wt_ev, 1)
                s.activation(woutT[d][:, :, :], psH[:, 6 * P:8 * P], ACT.Copy).then_inc(wt_ev, 1)
            act_e.wait_ge(halved, 7)

            def exps(step, b, d, n):
                wait(act_e, h_s, step)
                lo, hi, first = (1, T, 0) if d == 0 else (0, T - 1, T - 1)
                decay = psA[:, :].rearrange("p (k t) -> p k t", t=T)
                if n == 0:
                    act_e.wait_ge(dt_s, 2 * b + d + 1)
                    s.activation(decay[:, :, first:first + 1], zero[:, :, :], ACT.Copy).then_inc(a_s, 1)
                for half in range(NH):
                    s.activation(decay[:, half, lo:hi], dt_[d][:, half, lo:hi], ACT.Exp,
                                 scale=aneg[d][:, half, n:n + 1]).then_inc(a_s, 1)

            def take(b, pos):
                act_e.wait_ge(pP_full, PIECES * b + pos + 1)

            def silu(b, d, kind, half):
                k = 8 * b + 4 * d + kind + half
                at = kind + half
                take(b, piece(d, kind, half))
                wait(act_e, silu_s, k - 3)
                if kind == U:
                    s.activation(xh[:, at, :], psP[:, :], ACT.Identity, scale=0.5,
                                 bias=convb[d][:, half:half + 1]).then_inc(pP_free, 1)
                else:
                    s.activation(xh[:, at, :], psP[:, :], ACT.Copy, scale=0.5).then_inc(pP_free, 1)
                act_e.wait_ge(pP_free, PIECES * b + piece(d, kind, half) + 1)
                s.activation(th[:, at, :], xh[:, at, :], ACT.Tanh).then_inc(th_s, 1)

            def prep(b, d, k):
                if k - U_AT in (1, 3):
                    silu(b, d, U, (k - U_AT) // 2)
                if k == XD_AT:
                    take(b, piece(d, XD))
                    wait(act_e, brow_out, 16 * (2 * b + d))
                    s.activation(xd[:, :], psP[0:R + N, :], ACT.Copy).then_inc(pP_free, 1)
                if k == CP_AT:
                    take(b, piece(d, CP))
                    s.activation(cc[d][:, :, :], psP[:, 0:NT * N], ACT.Copy).then_inc(pP_free, 1)
                if k - DT_AT in (0, 1):
                    half = k - DT_AT
                    q = 5 * (2 * b + d)
                    take(b, piece(d, DT, half))
                    wait(act_e, dt_s, 2 * b + d)
                    s.activation(ab[:, half, :], psP[:, :], ACT.Abs, bias=bdt[d][:, half:half + 1]).then_inc(sp_s, 1)
                    s.activation(xb[:, half, :], psP[:, :], ACT.Relu,
                                 bias=bdt[d][:, half:half + 1]).then_inc(pP_free, 1)
                    act_e.wait_ge(sp_s, q + 2 * half + 1)
                    s.activation(ab[:, half, :], ab[:, half, :], ACT.Exp, scale=-1.0).then_inc(sp_s, 1)
                if k - Z_AT in (0, 1):
                    silu(b, d, Z, k - Z_AT)

            def ln1p(b, d):
                act_e.wait_ge(sp_s, 5 * (2 * b + d) + 4)
                s.activation(ab[:, :, :], ab[:, :, :], ACT.Ln, bias=1.0).then_inc(sp_s, 1)

            def side(b, slot, prep_b, prep_f):
                if prep_f is not None:
                    if slot == XN_SLOT:
                        act_e.wait_ge(pP_full, xn_piece(prep_f) + 1)
                        s.activation(xnT[:, PAD:PAD + T], psP[:, :], ACT.Identity, scale=norm[:, 0:1],
                                     bias=norm[:, 1:2]).then_inc(pP_free, 1)
                    prep(prep_f, 0, slot - PREP_SLOT[0])
                if prep_b:
                    prep(b, 1, slot - PREP_SLOT[1])

            def ffn_side(fb, slot):
                if slot == H2T_SLOT:
                    act_e.wait_ge(F2_full, (DOWN + NE) * fb + H2T + 1)
                    act_e.wait_ge(modF_in, 48 * fb + 48)
                    s.activation(h2T[:, :], F2[:, :], ACT.Identity, scale=modC[:, 1:2], bias=modC[:, 0:1])\
                        .then_inc(F2_free, 1)
                if slot == GATE_SLOT + 2:
                    act_e.wait_ge(gate_s, GATES * fb + GATE_D)
                    s.activation(ge[:, :], gd[:, :], ACT.Exp).then_inc(ge_s, 1)
                k = up_at(slot)
                if k is not None:
                    at = 2 * NE * fb + k
                    act_e.wait_ge(F0_full, at + 1)
                    wait(act_e, pf_s, at - 1)
                    s.activation(tf[:, k % 2, :], F0[:, :], ACT.Tanh, scale=0.5).then_inc(F0_free, 1)
                    s.activation(hf[:, k % 2, :], F0[:, :], ACT.Copy).then_inc(F0_free, 1)
                    act_e.wait_ge(F1_full, at + 1)
                    wait(act_e, act_s, at - 2)
                    s.activation(gf[:, k % 3, :], F1[:, :], ACT.Copy).then_inc(F1_free, 1)
                if down_at(slot) == (0, 1):
                    act_e.wait_ge(F2_full, (DOWN + NE) * fb + DOWN + 1)
                    wait(act_e, o_s, 2 * fb)
                    s.activation(facc[:, :, :], F2[:, :], ACT.Copy).then_inc(F2_free, 1)

            for slot in range(STEPS):
                side(-1, slot, False, 0)
                if slot == PREP_SLOT[0] + LN1P_AT:
                    ln1p(0, 0)
            act_e.wait_ge(const_ok, CONSTS)
            exps(0, 0, 0, 0)

            def body(b, scan, ffn, last):
                for slot in range(STEPS):
                    nxt = slot + 1
                    if scan and nxt < STEPS:
                        exps(STEPS * b + nxt, b, nxt // N, nxt % N)
                    elif scan and not last:
                        exps(STEPS * b + nxt, b + 1, 0, 0)
                    if scan and not last and slot == PREP_SLOT[0] + LN1P_AT:
                        ln1p(b + 1, 0)
                    if scan and slot == PREP_SLOT[1] + LN1P_AT:
                        ln1p(b, 1)
                    if scan:
                        if slot == FX_SLOT + 2:
                            wait(act_e, F2_free, (DOWN + 1) * (b - 1) + PROJ + 1)
                            act_e.wait_ge(h1_s, 2 * b + 2)
                            s.activation(h1K[:, :, :], z1[:, :, :], ACT.Copy).then_inc(h1K_s, 1)
                    if ffn:
                        ffn_side(b - 1, slot)
                    if scan:
                        side(b, slot, True, None if last else b + 1)

            passes(act_e, body)

        @block.vector
        def _(dve):
            w = nc.vector
            w.memset(xnT[:, 0:PAD], 0.0).then_inc(const_ok, 1)
            w.memset(xnT[:, PAD + T:], 0.0).then_inc(const_ok, 1)
            w.memset(zero[:, :, :], 0.0).then_inc(const_ok, 1)
            dve.wait_ge(c_step, 1)
            w.scalar_tensor_tensor(c_silu[:, :], c_th[:, :], 1.0, c_nat[:, :], ALU.add, ALU.mult).then_inc(c_step, 1)
            dve.wait_ge(mod_mm, 1)
            for k in range(KINDS):
                src = (F0, F1)[k // 4][0:NB, (k % 4) * D:(k % 4) * D + D]
                w.tensor_scalar(mod[:, k, :], src, 0.5, 1.0 if k % 3 == 1 else 0.0, ALU.mult, ALU.add)\
                    .then_inc(mod_v, 1)
            dve.wait_ge(mod_v, KINDS)
            gates = mod[:, 2:6:3, :]
            w.tensor_scalar(gsgn[:, :, :], gates, 0.0, 2.0, ALU.is_ge, ALU.mult).then_inc(mod_v, 1)
            w.scalar_tensor_tensor(gabs[:, :, :], gates, -1.0, gates, ALU.mult, ALU.max).then_inc(mod_v, 1)
            dve.wait_ge(mod_v, KINDS + 2)
            w.tensor_scalar(gabs[:, :, :], gabs[:, :, :], 0.25, None, ALU.max).then_inc(mod_v, 1)
            w.tensor_scalar(gsgn[:, :, :], gsgn[:, :, :], -1.0, None, ALU.add).then_inc(mod_v, 1)
            dve.wait_ge(mod_v, KINDS + 4)
            for k in range(2):
                w.tensor_tensor(mod[:, 2 + 3 * k, :], gsgn[:, k, :], gabs[:, k, :], ALU.mult).then_inc(mod_v, 1)
            dve.wait_ge(loaded, LOADS)
            for d in range(2):
                for half in range(NH):
                    for j in range(TAPS):
                        w.tensor_scalar(win_tap[d][:, half, j, :], win_nat[d][:, half, :],
                                        convw[d][:, half, j:j + 1], None, ALU.mult).then_inc(taps_ok, 1)
            dve.wait_ge(ident_ok, 2)
            for d in range(2):
                for half in range(NH):
                    w.tensor_scalar(diag[:, d, half, :], ident[:, :], skip[d][:, half:half + 1], None, ALU.mult)\
                        .then_inc(diag_ok, 1)
            dve.wait_ge(mod_v, MOD_STEPS)

            def scan(step, d, n, unit):
                dve.wait_ge(a_s, NH * (step + 1) + unit)
                dve.wait_ge(bt_s, step + 1)
                wait(dve, pH_full, 2 * step - 2)
                order = slice(None) if d == 0 else slice(None, None, -1)
                w.tensor_tensor_scan(h[:, n % 2, :, :].rearrange("p k t -> p (k t)")[:, order], psA[:, order],
                                     bt[:, n % 2, :, :].rearrange("p k t -> p (k t)")[:, order],
                                     0.0, ALU.mult, ALU.add).then_inc(h_s, 1)

            def read_out(step, d, n, b):
                wait(dve, acc_s, NT * step)
                if n == 0:
                    if d == 0:
                        wait(dve, pP_full, post_piece(b - 1, NH))
                    else:
                        wait(dve, F2_full, (DOWN + NE) * (b - 1) + POSTB + NH)
                for i in range(NT):
                    if i % 2 == 0:
                        dve.wait_ge(pH_full, 2 * step + 1 + i // 2)
                    dst, src = acc[d][:, i, :], psH[:, i * E:i * E + E]
                    c = cc[d][:, i, n:n + 1]
                    if n == 0:
                        w.tensor_scalar(dst, src, c, None, ALU.mult).then_inc(acc_s, 1)
                    else:
                        w.scalar_tensor_tensor(dst, src, c, dst, ALU.mult, ALU.add).then_inc(acc_s, 1)

            def statistics(x_, st_, sig):
                for i in range(NT):
                    w.bn_stats(st_[:, i, :], x_[:, i, :]).then_inc(sig, 1)

            def normalize(dst, x_, stat_, rstd_, sig):
                for i in range(NT):
                    w.tensor_scalar(dst[:, i, :], x_[:, i, :], stat_[:, i, 0:1], rstd_[:, i:i + 1],
                                    ALU.subtract, ALU.mult).then_inc(sig, 1)

            def norms(b, slot):
                if slot == LN_SLOT:
                    dve.wait_ge(x_in, 16 * b + 16)
                    wait(dve, rstdA, 14 * b)
                    statistics(x, st, lnA)
                if slot == LN_SLOT + 2:
                    dve.wait_ge(rstdA, 14 * b + 7)
                    wait(dve, h1K_s, b)
                    normalize(z1, x, stat, rstd, zA)
                if slot == LN_SLOT + 4:
                    dve.wait_ge(h1_s, 2 * b + 2)
                    statistics(z1, st, lnA)
                if slot == LN_SLOT + 6:
                    dve.wait_ge(rstdA, 14 * b + 14)
                    normalize(xn, z1, stat, rstd, zA)

            def silu(b, d, kind, half):
                k = 8 * b + 4 * d + kind + half
                dve.wait_ge(th_s, k + 1)
                if d == 0:
                    wait(dve, pP_full, post_piece(b - 1, half) + 1)
                else:
                    wait(dve, F2_full, (DOWN + NE) * (b - 1) + POSTB + half + 1)
                dst = (u if kind == U else zs)[d][:, half, :]
                w.scalar_tensor_tensor(dst, th[:, kind + half, :], 1.0, xh[:, kind + half, :], ALU.add, ALU.mult).then_inc(silu_s, 1)

            def prep(b, d, k):
                if k - U_AT in (3, 5):
                    silu(b, d, U, (k - U_AT - 3) // 2)
                if k - Z_AT in (2, 3):
                    silu(b, d, Z, k - Z_AT - 2)

            def gate_y(b, d, half):
                if d == 0:
                    dve.wait_ge(pP_full, post_piece(b, half) + 1)
                    wait(dve, F2_full, (DOWN + NE) * (b - 1) + PROJ + 1)
                    src, sig = psP, pP_free
                else:
                    dve.wait_ge(F2_full, (DOWN + NE) * b + POSTB + half + 1)
                    src, sig = F2, F2_free
                dve.wait_ge(silu_s, 8 * b + 4 * d + 4)
                w.tensor_tensor(yg[d][:, half, :], src[:, :], zs[d][:, half, :], ALU.mult).then_inc(sig, 1)

            def gate(fb):
                q = GATES * fb
                dve.wait_ge(F2_full, (DOWN + NE) * fb + GATE + 1)
                w.tensor_copy(gl[:, :, :], F2[:, 0:NT * NX]).then_inc(F2_free, 1)
                dve.wait_ge(F2_free, (DOWN + 1) * fb + GATE + 1)
                w.tensor_copy(gl2[:, :, :], gl[:, :, :]).then_inc(gate_s, 1)
                for i in range(NT):
                    w.max(top[:, i, :], gl[:, i, :]).then_inc(gate_s, 1)
                dve.wait_ge(gate_s, q + 5)
                w.tensor_tensor(gd[:, :], top[:, :, 1], top[:, :, 0], ALU.subtract).then_inc(gate_s, 1)
                for i in range(NT):
                    w.max_index(topi[:, i, :], top[:, i, :], gl2[:, i, :]).then_inc(gate_s, 1)
                dve.wait_ge(gate_s, q + 10)
                w.tensor_copy(topf[:, :, :], topi[:, :, 0:2]).then_inc(gate_s, 1)
                dve.wait_ge(gate_s, q + 11)
                wait(dve, wts_s, 3 * fb)
                for j in range(2):
                    w.tensor_tensor(hot[:, j, :, :], iota8[:, :].unsqueeze(1).broadcast_to([P, NT, NX]),
                                    topf[:, :, j:j + 1].broadcast_to([P, NT, NX]), ALU.is_equal).then_inc(gate_s, 1)

            def gate_weights(fb):
                q = 3 * fb
                wait(dve, wts_s, 3 * fb)
                dve.wait_ge(ge_s, fb + 1)
                w.tensor_scalar(gs[:, :], ge[:, :], 1.0, None, ALU.add).then_inc(gw_s, 1)
                dve.wait_ge(gw_s, q + 1)
                w.reciprocal(gw[:, 0, :], gs[:, :]).then_inc(gw_s, 1)
                dve.wait_ge(gw_s, q + 2)
                w.tensor_tensor(gw[:, 1, :], gw[:, 0, :], ge[:, :], ALU.mult).then_inc(gw_s, 1)

            def expert_silu(fb, slot):
                k = up_at(slot - 1)
                if k is not None:
                    at = 2 * NE * fb + k
                    dve.wait_ge(F0_free, 2 * at + 2)
                    wait(dve, act_s, at - 1)
                    w.scalar_tensor_tensor(pf[:, k % 2, :], tf[:, k % 2, :], 1.0, hf[:, k % 2, :],
                                           ALU.add, ALU.mult).then_inc(pf_s, 1)

            def expert_sum(fb, slot):
                down = down_at(slot)
                if down and down[0] and down[1]:
                    e = down[0]
                    dve.wait_ge(F2_full, (DOWN + NE) * fb + DOWN + e + 1)
                    if e == 1:
                        dve.wait_ge(F2_free, (DOWN + 1) * fb + DOWN + 1)
                        dve.wait_ge(wts_s, 3 * fb + 3)
                    wait(dve, facc_s, NX * NT * fb + NT * (e - 1))
                    for i in range(NT):
                        w.scalar_tensor_tensor(facc[:, i, :], F2[:, i * D:i * D + D],
                                               wts[:, i, ORDER[e]:ORDER[e] + 1], facc[:, i, :],
                                               ALU.mult, ALU.add).then_inc(facc_s, 1)

            def ffn_side(fb, slot):
                if slot - POSTB_SLOT in (0, 1):
                    gate_y(fb, 1, slot - POSTB_SLOT)
                if slot == FX_SLOT:
                    dve.wait_ge(F2_full, (DOWN + NE) * fb + PROJ + 1)
                    dve.wait_ge(h1K_s, fb + 1)
                    wait(dve, o_s, 2 * fb)
                    w.tensor_tensor(fx[:, :, :], F2[:, :].rearrange("p (k c) -> p k c", c=D), h1K[:, :, :], ALU.add)\
                        .then_inc(F2_free, 1)
                if slot == LN3_SLOT:
                    dve.wait_ge(x2_s, 2 * fb + 2)
                    wait(dve, rstdF_s, 7 * fb)
                    statistics(x2, stF, lnF)
                if slot == LN3_SLOT + 1:
                    dve.wait_ge(rstdF_s, 7 * fb + 7)
                    wait(dve, F2_full, (DOWN + NE) * fb)
                    normalize(zF, x2, statF, rstdF, zF_s)
                if slot == GATE_SLOT + 1:
                    gate(fb)
                if slot == GATE_SLOT + 3:
                    gate_weights(fb)

            def side(b, slot, prep_b, prep_f, post_f):
                if prep_f is not None:
                    norms(prep_f, slot)
                    prep(prep_f, 0, slot - PREP_SLOT[0])
                if prep_b:
                    prep(b, 1, slot - PREP_SLOT[1])

            for slot in range(STEPS):
                side(-1, slot, False, 0, False)
            dve.wait_ge(const_ok, CONSTS)

            def body(b, scan_, ffn, last):
                for slot in range(STEPS):
                    step = STEPS * b + slot
                    if scan_:
                        scan(step, slot // N, slot % N, 2 * b + 1 + slot // N)
                    if ffn:
                        expert_silu(b - 1, slot)
                    if slot > 0 and scan_:
                        read_out(step - 1, (slot - 1) // N, (slot - 1) % N, b)
                    elif slot == 0 and ffn:
                        read_out(step - 1, 1, N - 1, b - 1)
                    if scan_:
                        side(b, slot, True, None if last else b + 1, True)
                    if ffn:
                        ffn_side(b - 1, slot)
                        expert_sum(b - 1, slot)
                    if scan_ and slot - POST_F_SLOT in (0, 1):
                        gate_y(b, 0, slot - POST_F_SLOT)

            passes(dve, body)

        @block.tensor
        def _(pe):
            m = nc.tensor
            pe.wait_ge(ident_ok, 2)
            pe.wait_ge(c_step, 2)
            m.transpose(F0[:, 0:NB], c_silu[:, :], ident[0:NB, 0:NB]).then_inc(c_step, 1)
            pe.wait_ge(c_step, 4)
            m.matmul(F0[0:NB, :], cT[:, :], wmod[:, 0:T], start=True, stop=True)
            m.matmul(F1[0:NB, 0:2 * D], cT[:, :], wmod[:, T:KINDS * D], start=True, stop=True).then_inc(mod_mm, 1)
            pe.wait_ge(loaded, LOADS)
            for d in range(2):
                pe.wait_ge(taps_ok, NH * TAPS * (d + 1))
                if d:
                    pe.wait_ge(wt_ev, 5)
                for half in range(NH):
                    for j in range(TAPS):
                        col = (half * TAPS + j) * P
                        m.transpose(psA[:, col:col + P], win_tap[d][:, half, j, :], ident[:, :])
                    m.transpose(psH[:, half * P:half * P + P], win_nat[d][:, NH + half, :], ident[:, :])
                    k = R + 2 * N
                    m.transpose(psH[:, (2 + half) * P:(2 + half) * P + k], wx_nat[d][:, half * P:half * P + P],
                                ident[0:k, 0:k])
                    m.transpose(psH[0:R, (4 + half) * P:(5 + half) * P], wdt_nat[d][:, half, :], ident[:, :])
                    last = m.transpose(psH[:, (6 + half) * P:(7 + half) * P], wout_nat[d][:, half * P:half * P + P],
                                       ident[:, :])
                last.then_inc(wt_tr, 1)
            pe.wait_ge(mod_v, KINDS)
            pe.wait_ge(diag_ok, 2 * NH)
            pe.wait_ge(wt_ev, 10)
            pe.wait_ge(halved, 7)

            def tr_h(step, n):
                pe.wait_ge(h_s, step + 1)
                for i in range(NT):
                    if i % 2 == 0:
                        wait(pe, acc_s, NT * step - NT + i + 2)
                    for half in range(NH):
                        last = m.transpose(psH[:, i * E + half * P:i * E + half * P + P],
                                           h[:, n % 2, half, i * P:i * P + P], ident[:, :])
                    if i % 2 == 1:
                        last.then_inc(pH_full, 1)

            def prep(b, d, k):
                def open_piece(kind, half=0):
                    wait(pe, pP_free, PIECES * b + piece(d, kind, half))
                if 0 <= k - U_AT < 2 * NH:
                    half, late = divmod(k - U_AT, 2)
                    if not late:
                        open_piece(U, half)
                    for j in (2, 3) if late else (0, 1):
                        lo = j if d == 0 else 2 * PAD - j
                        last = m.matmul(psP[:, :], wcT[d][:, half, j, :], xnT[:, lo:lo + T],
                                        start=(j == 0), stop=(j == TAPS - 1))
                    if late:
                        last.then_inc(pP_full, 1)
                    return
                if k == XD_AT:
                    pe.wait_ge(silu_s, 8 * b + 4 * d + 2)
                    open_piece(XD)
                    for half in range(NH):
                        last = m.matmul(psP[0:R + N, :], wxT[d][:, half, 0:R + N], u[d][:, half, :],
                                        start=(half == 0), stop=(half == NH - 1))
                    last.then_inc(pP_full, 1)
                if k == CP_AT:
                    open_piece(CP)
                    for i in range(NT):
                        for half in range(NH):
                            last = m.matmul(psP[:, i * N:(i + 1) * N], u[d][:, half, i * P:i * P + P],
                                            wxT[d][:, half, R + N:R + 2 * N], start=(half == 0), stop=(half == NH - 1))
                    last.then_inc(pP_full, 1)
                if k - DT_AT in (0, 1):
                    open_piece(DT, k - DT_AT)
                    m.matmul(psP[:, :], wdtT[d][:, k - DT_AT, :], xd[0:R, :], start=True, stop=True).then_inc(pP_full, 1)
                if k - Z_AT in (0, 1):
                    open_piece(Z, k - Z_AT)
                    m.matmul(psP[:, :], wzT[d][:, k - Z_AT, :], xnT[:, PAD:PAD + T], start=True, stop=True)\
                        .then_inc(pP_full, 1)

            def skip_and_turn(bank, d, half):
                m.matmul(bank[:, :], diag[:, d, half, :], u[d][:, half, :], start=True, stop=False)
                for i in range(NT):
                    last = m.matmul(bank[:, i * P:i * P + P], acc[d][:, i, half * P:half * P + P], ident[:, :],
                                    start=False, stop=(i == NT - 1))
                return last

            def side(b, slot, prep_b, prep_f, post_f):
                if post_f and slot in (POST_F_SLOT, POST_F_SLOT + 1):
                    half = slot - POST_F_SLOT
                    pe.wait_ge(acc_s, NT * (STEPS * b + N))
                    wait(pe, pP_free, post_piece(b, half))
                    skip_and_turn(psP, 0, half).then_inc(pP_full, 1)
                if prep_f is not None:
                    if slot == XN_SLOT:
                        pe.wait_ge(zA, 8 * prep_f + 8)
                        wait(pe, pP_free, xn_piece(prep_f))
                        for i in range(NT):
                            last = m.transpose(psP[:, i * P:i * P + P], xn[:, i, :], ident[:, :])
                        last.then_inc(pP_full, 1)
                    prep(prep_f, 0, slot - PREP_SLOT[0])
                if prep_b:
                    prep(b, 1, slot - PREP_SLOT[1])

            def ffn_side(fb, slot):
                free = (DOWN + 1) * fb
                if slot - POSTB_SLOT in (0, 1):
                    half = slot - POSTB_SLOT
                    if half == 0:
                        pe.wait_ge(acc_s, NT * (STEPS * fb + STEPS))
                        wait(pe, facc_s, NX * NT * fb)
                    else:
                        pe.wait_ge(F2_free, free + POSTB + half)
                    skip_and_turn(F2, 1, half).then_inc(F2_full, 1)
                k = up_at(slot)
                if k is not None:
                    x_, half = ORDER[k // 2], k % 2
                    at = 2 * NE * fb + k
                    if k == 0:
                        pe.wait_ge(F2_free, free + H2T + 1)
                    wait(pe, F0_free, 2 * at)
                    m.matmul(F0[:, :], w1[:, x_, half * P:half * P + P], h2T[:, :], start=True, stop=True)\
                        .then_inc(F0_full, 1)
                    wait(pe, F1_free, at)
                    m.matmul(F1[:, :], w2[:, x_, half * P:half * P + P], h2T[:, :], start=True, stop=True)\
                        .then_inc(F1_full, 1)

            def ffn_late(fb, slot):
                free = (DOWN + 1) * fb
                if slot - PROJ_SLOT in (0, 1):
                    if slot == PROJ_SLOT:
                        pe.wait_ge(pP_free, post_piece(fb, NH))
                        pe.wait_ge(F2_free, free + PROJ)
                    for i in (0, 1) if slot == PROJ_SLOT else (2, 3):
                        for k in range(2 * NH):
                            last = m.matmul(F2[:, i * D:i * D + D], yg[k // NH][:, k % NH, i * P:i * P + P],
                                            woutT[k // NH][:, k % NH, :], start=(k == 0), stop=(k == 2 * NH - 1))
                    if slot == PROJ_SLOT + 1:
                        last.then_inc(F2_full, 1)
                if slot == H2T_SLOT:
                    pe.wait_ge(zF_s, NT * fb + NT)
                    pe.wait_ge(F2_free, free + H2T)
                    for i in range(NT):
                        last = m.transpose(F2[:, i * P:i * P + P], zF[:, i, :], ident[:, :])
                    last.then_inc(F2_full, 1)
                if slot == GATE_SLOT:
                    pe.wait_ge(F2_free, free + GATE)
                    for i in range(NT):
                        last = m.matmul(F2[:, i * NX:(i + 1) * NX], h2T[:, i * P:i * P + P], gate_w[:, :],
                                        start=True, stop=True)
                    last.then_inc(F2_full, 1)
                down = down_at(slot)
                if down:
                    e, part = down
                    if part == 0:
                        pe.wait_ge(act_s, 2 * NE * fb + 2 * e + 2)
                        if e <= 1:
                            pe.wait_ge(F2_free, free + DOWN + e)
                        else:
                            pe.wait_ge(facc_s, NX * NT * fb + NT * (e - 1))
                    for i in (2 * part, 2 * part + 1):
                        for half in range(2):
                            last = m.matmul(F2[:, i * D:i * D + D], act[:, e % 3, half, i * P:i * P + P],
                                            w3[:, ORDER[e], half, :], start=(half == 0), stop=(half == 1))
                    if part == 1:
                        last.then_inc(F2_full, 1)

            for slot in range(STEPS):
                side(-1, slot, False, 0, False)

            def body(b, scan_, ffn, last):
                for slot in range(STEPS):
                    step = STEPS * b + slot
                    if (slot > 0 and scan_) or (slot == 0 and ffn):
                        tr_h(step - 1, (slot - 1) % N)
                    if ffn:
                        ffn_side(b - 1, slot)
                        ffn_late(b - 1, slot)
                    if scan_:
                        side(b, slot, True, None if last else b + 1, True)

            passes(pe, body)


_NAMES = {
    "L0_attn_x": "x", "L0_attn_norm_g": "norm_g", "L0_attn_norm_b": "norm_b", "L0_ffn_gate_w": "gate_w",
    "L0_ffn_ew1": "ew1", "L0_ffn_ew2": "ew2", "L0_ffn_ew3": "ew3", "L0_ffn_sw1": "sw1", "L0_ffn_sw2": "sw2",
    "L0_ffn_sw3": "sw3", "L0_c": "c", "L0_wmod": "wmod",
}
_DIR = ["Win", "convw", "convb", "Wx", "Wdt", "bdt", "Alog", "D", "Wout"]


def kernel(**inputs):
    import numpy as _np
    import concourse.bacc as _bacc
    from concourse import mybir as _mybir
    from concourse.bass_utils import run_bass_kernel_spmd as _run

    nc = _bacc.Bacc("TRN2", target_bir_lowering=False, num_devices=1)
    arrays = {}

    def given(name):
        arr = _np.ascontiguousarray(inputs[name])
        arrays[f"in_{name}"] = arr
        return nc.dram_tensor(f"in_{name}", arr.shape, _mybir.dt.from_np(arr.dtype), kind="ExternalInput").ap()

    t = {short: given(name) for name, short in _NAMES.items()}
    for d in "fb":
        t[d] = {w: given(f"L0_attn_{d}_{w}") for w in _DIR}
    out = nc.dram_tensor("out_x", (NB, T, D), _mybir.dt.float32, kind="ExternalOutput").ap()
    adaln_mamba_moe(nc, t, out)
    r = _run(nc, [arrays], core_ids=[0])
    return r.results[0]["out_x"]
```
